# Optimizing a Trainium2 kernel written in Bass

```python
import numpy as np
import jax
import jax.numpy as jnp

def _softmax(x, axis=-1):
    return jax.nn.softmax(x, axis=axis)

def _gelu(x):
    return jax.nn.gelu(x, approximate=True)

def _silu(x):
    return jax.nn.silu(x)

def _sigmoid(x):
    return jax.nn.sigmoid(x)

def _layernorm(x, axis=-1, eps=1e-05):
    m = jnp.mean(x, axis=axis, keepdims=True)
    v = jnp.var(x, axis=axis, keepdims=True)
    return (x - m) / jnp.sqrt(v + eps)

def _scatter_add(tgt, idx, src, axis=0):
    return tgt.at[idx].add(src)

def _segment_sum(src, seg, n):
    return jax.ops.segment_sum(src, seg, n)
kernel_name = 'mk_flamingo_gated_d1_seqx_r8_f2f428'

def setup_inputs(seed: int=0):
    np.random.seed(seed)
    _w = jnp.asarray

    def _rec_inputs():
        import jax
        import jax.numpy as jnp
        _rk = jax.random.key(seed)
        x = -0.000125 + 0.9999 * jax.random.normal(jax.random.fold_in(_rk, 1), (4, 256, 256), jnp.float32)
        _lenS = 256 - jax.random.randint(jax.random.fold_in(_rk, 7), (4,), 0, max(1, 256 // 4) + 1, jnp.int32)
        _lenS2 = 256 - jax.random.randint(jax.random.fold_in(_rk, 8), (4,), 0, max(1, 256 // 4) + 1, jnp.int32)
        itok_BxS_13_99985 = jax.random.randint(jax.random.fold_in(_rk, 11), (4, 256), 13, 99986, jnp.int32)
        _ctx_2048P = jax.random.normal(jax.random.fold_in(_rk, 12), (4, 16, 256), jnp.float32)
        _ctx_2048c = jax.random.dirichlet(jax.random.fold_in(_rk, 512), 0.3 * jnp.ones((16,), jnp.float32), (4, 256))
        _ctx_2048t = jnp.einsum('bsk,bkd->bsd', _ctx_2048c, _ctx_2048P)
        _ctx_2048t = _ctx_2048t * jax.lax.rsqrt(jnp.mean(jnp.square(_ctx_2048t)) + 1e-12) * 0.953939
        ctx_2048 = 6.82029e-06 + 0.0200006 * (_ctx_2048t + 0.3 * jax.random.normal(jax.random.fold_in(_rk, 612), (4, 256, 256), jnp.float32))
        _g = jax.random.normal(jax.random.fold_in(_rk, 9001), (2, 1), jnp.float32)
        _g = jnp.sign(_g) * jnp.maximum(jnp.abs(_g), 1.0) + (_g == 0) * 1.0
        g_xattn = _g[0]
        g_ffn = _g[1]
        return (x, itok_BxS_13_99985, ctx_2048, g_xattn, g_ffn)
    x, itok_BxS_13_99985, ctx_2048, g_xattn, g_ffn = _rec_inputs()

    def _L0_xattn_setup():
        import jax, jax.numpy as jnp
        import numpy as np
        B, S, D = (4, 512, 256)
        E = 4
        F = 1024 // E
        VOCAB = 12500
        key = jax.random.key(seed)
        k1, k2, k3, k4, k5 = jax.random.split(key, 5)
        hidden_states = jax.random.normal(k1, (B, S, D), dtype=jnp.float32)
        token_ids = jax.random.randint(k2, (B, S), 0, VOCAB, dtype=jnp.int64)
        Wg = jax.random.normal(k3, (E, F, D), dtype=jnp.float32) * 0.02
        Wu = jax.random.normal(k4, (E, F, D), dtype=jnp.float32) * 0.02
        Wd = jax.random.normal(k5, (E, D, F), dtype=jnp.float32) * 0.02
        return {'hidden_states': hidden_states, 'token_ids': token_ids, 'Wg': Wg, 'Wu': Wu, 'Wd': Wd}
    _L0_xattn_all = _L0_xattn_setup()
    _L0_xattn_in = {k: v for k, v in _L0_xattn_all.items() if k in ()}
    del _L0_xattn_all

    def _L0_ffn_setup():
        import jax, jax.numpy as jnp
        import numpy as np
        LN_EPS = 1e-05
        L2_EPS = 1e-12

        def _l2norm(v, axis):
            n = jnp.sqrt(jnp.sum(v * v, axis=axis, keepdims=True))
            return v / jnp.maximum(n, L2_EPS)
        key = jax.random.key(seed)
        ks = jax.random.split(key, 4)
        B, N, D, E, S, H = (8, 256, 256, 16, 128, 64)
        x = jax.random.normal(ks[0], (B, N, D), dtype=jnp.float32)
        mu = jax.random.normal(ks[1], (D, E, S), dtype=jnp.float32) / np.sqrt(D)
        W1 = jax.random.normal(ks[2], (E, D, H), dtype=jnp.float32) * np.sqrt(2.0 / D)
        W2 = jax.random.normal(ks[3], (E, H, D), dtype=jnp.float32) * np.sqrt(2.0 / (H + D))
        return {'x': x, 'gamma': jnp.ones((D,), jnp.float32), 'beta': jnp.zeros((D,), jnp.float32), 'mu': mu, 'scale': jnp.ones((1,), jnp.float32), 'W1': W1, 'b1': jnp.zeros((E, H), jnp.float32), 'W2': W2, 'b2': jnp.zeros((E, D), jnp.float32)}
    _L0_ffn_all = _L0_ffn_setup()
    _L0_ffn_in = {k: v for k, v in _L0_ffn_all.items() if k in ('gamma', 'beta', 'mu', 'scale', 'W1', 'b1', 'W2', 'b2')}
    del _L0_ffn_all
    return {'x': x, 'itok_BxS_13_99985': itok_BxS_13_99985, 'ctx_2048': ctx_2048, 'g_xattn': g_xattn, 'g_ffn': g_ffn, 'L0_ffn_gamma': _L0_ffn_in['gamma'], 'L0_ffn_beta': _L0_ffn_in['beta'], 'L0_ffn_mu': _L0_ffn_in['mu'], 'L0_ffn_scale': _L0_ffn_in['scale'], 'L0_ffn_W1': _L0_ffn_in['W1'], 'L0_ffn_b1': _L0_ffn_in['b1'], 'L0_ffn_W2': _L0_ffn_in['W2'], 'L0_ffn_b2': _L0_ffn_in['b2']}

def reference(x, itok_BxS_13_99985, ctx_2048, g_xattn, g_ffn, L0_ffn_gamma, L0_ffn_beta, L0_ffn_mu, L0_ffn_scale, L0_ffn_W1, L0_ffn_b1, L0_ffn_W2, L0_ffn_b2):
    import jax
    import jax.numpy as jnp

    def _L0_xattn_ref(hidden_states, token_ids, Wg, Wu, Wd):
        import jax, jax.numpy as jnp
        import numpy as np
        B, S, D = (4, 512, 256)
        E = 4
        F = 1024 // E
        VOCAB = 12500
        tokens_per_expert = VOCAB // E
        tid = jnp.clip(token_ids, 0, VOCAB - 1)
        expert_ids = jnp.minimum(tid // tokens_per_expert, E - 1)
        out = jnp.zeros_like(hidden_states)
        for e in range(E):
            g = jax.nn.silu(jnp.einsum('bsd,fd->bsf', hidden_states, Wg[e]))
            u = jnp.einsum('bsd,fd->bsf', hidden_states, Wu[e])
            y = jnp.einsum('bsf,df->bsd', g * u, Wd[e])
            out = jnp.where((expert_ids == e)[..., None], y, out)
        return out

    def _L0_ffn_ref(x, gamma, beta, mu, scale, W1, b1, W2, b2):
        import jax, jax.numpy as jnp
        import numpy as np
        LN_EPS = 1e-05
        L2_EPS = 1e-12

        def _l2norm(v, axis):
            n = jnp.sqrt(jnp.sum(v * v, axis=axis, keepdims=True))
            return v / jnp.maximum(n, L2_EPS)
        B, N, D = x.shape
        _, E, S = mu.shape
        mean = jnp.mean(x, axis=-1, keepdims=True)
        var = jnp.mean(jnp.square(x - mean), axis=-1, keepdims=True)
        x_ln = (x - mean) / jnp.sqrt(var + LN_EPS) * gamma + beta
        x_n = _l2norm(x_ln, -1) * scale
        mu_n = _l2norm(mu, 0)
        logits = jnp.einsum('bnd,des->bnes', x_n, mu_n)
        dispatch = jax.nn.softmax(logits, axis=1)
        combine = jax.nn.softmax(logits.reshape(B, N, E * S), axis=-1)
        slot_in = jnp.einsum('bnd,bnes->besd', x_ln, dispatch)
        h = jax.nn.gelu(jnp.einsum('besd,edh->besh', slot_in, W1) + b1[None, :, None, :], approximate=False)
        slot_out = jnp.einsum('besh,ehd->besd', h, W2) + b2[None, :, None, :]
        out = jnp.einsum('bsd,bns->bnd', slot_out.reshape(B, E * S, D), combine)
        return out
    x = x + jnp.tanh(g_xattn[0]) * _L0_xattn_ref(_layernorm(x, axis=-1), itok_BxS_13_99985, ctx_2048, ctx_2048, ctx_2048)
    x = x + jnp.tanh(g_ffn[0]) * _L0_ffn_ref(_layernorm(x, axis=-1), L0_ffn_gamma, L0_ffn_beta, L0_ffn_mu, L0_ffn_scale, L0_ffn_W1, L0_ffn_b1, L0_ffn_W2, L0_ffn_b2)
    return x

_drawn_inputs = setup_inputs


def setup_inputs(seed=0):
    import zlib

    import numpy as np

    out = dict(_drawn_inputs(seed))
    spreads = {'L0_ffn_gamma': (1.0, 0.6),
     'L0_ffn_beta': (0.0, 0.75),
     'L0_ffn_b1': (0.0, 0.8),
     'L0_ffn_b2': (0.0, 0.337)}
    factors = {'L0_ffn_mu': 8.0, 'L0_ffn_W1': 4.477, 'L0_ffn_W2': 3.981}
    for name, (base, spread) in spreads.items():
        noise = np.random.default_rng([zlib.crc32(name.encode()), seed]).standard_normal(out[name].shape)
        drawn = base * np.exp(spread * noise) if base else spread * noise
        out[name] = jnp.asarray(drawn.astype(out[name].dtype))
    for name, factor in factors.items():
        out[name] = (out[name] * factor).astype(out[name].dtype)
    return out
```

```python
from contextlib import ExitStack

import concourse.bass as bass
from concourse import mybir

F32 = mybir.dt.float32
F32R = mybir.dt.float32r
I32 = mybir.dt.int32
U8 = mybir.dt.uint8
BF16 = mybir.dt.bfloat16
ALU = mybir.AluOpType
ACT = mybir.ActivationFunctionType
AX = mybir.AxisListType

P = 128
VOCAB = 12500
LN_EPS = 1e-5
L2_EPS = 1e-12


def nth(b, per_batch, j):
    return b * per_batch + (j + 1)


def flamingo_kernel(nc, x, ids, ctx, g_xattn, g_ffn, gamma, beta, mu, scale, W1, b1, W2, b2, out):
    B, N, D = x.shape
    E, F, _ = ctx.shape
    _, E2, S = mu.shape
    H = W1.shape[2]
    NT = N // P
    DK = D // P
    ES = E2 * S
    EH = E2 * H
    CW = 512
    NCH = ES // CW
    EPC = CW // S
    NG = E2 // 2
    PER_EXPERT = VOCAB // E
    assert (NT, DK, S, 2 * H, F, E, EPC) == (2, 2, P, P, D, 4, 4)

    es = ExitStack()
    with es:
        def sb(name, shape, dt=F32):
            return es.enter_context(nc.sbuf_tensor(name, shape, dt))

        def sem(name):
            return es.enter_context(nc.semaphore(name))

        x_all = sb("x_all", [P, B * NT, D])
        xc = sb("xc", [P, NT, D])
        hT_hi = sb("hT_hi", [P, DK * N], F32R)
        hT_lo = sb("hT_lo", [P, DK * N], F32R)
        ctxT_hi = sb("ctxT_hi", [P, DK, E * F], F32R)
        ctxT_lo = sb("ctxT_lo", [P, DK, E * F], F32R)
        act = sb("act", [P, 2, 2 * N])
        act_hi = sb("act_hi", [P, 2, 2 * N], F32R)
        act_lo = sb("act_lo", [P, 2, 2 * N], F32R)
        cls = sb("cls", [P, B * N], U8)
        mask = sb("mask", [P, E, N], BF16)
        xT_hi = sb("xT_hi", [P, DK * N], F32R)
        xT_lo = sb("xT_lo", [P, DK * N], F32R)
        mu_hi = sb("mu_hi", [P, DK, ES], F32R)
        mu_lo = sb("mu_lo", [P, DK, ES], F32R)
        w1_hi = sb("w1_hi", [P, DK, EH], F32R)
        w1_lo = sb("w1_lo", [P, DK, EH], F32R)
        w2_hi = sb("w2_hi", [P, NG, D], F32R)
        w2_lo = sb("w2_lo", [P, NG, D], F32R)
        b1_bc = sb("b1_bc", [P, EH])
        b2_pad = sb("b2_pad", [P, D])
        gam = sb("gam", [P, D])
        bet = sb("bet", [P, D])
        ident = sb("ident", [P, P])
        G = sb("G", [P, NT, EH])
        lg = sb("lg", [P, NT, ES])
        dT = sb("dT", [P, 2, EPC, N])
        disp = sb("disp", [P, 2, NT, CW])
        cT_hi = sb("cT_hi", [P, 4, 2, N], F32R)
        cT_lo = sb("cT_lo", [P, 4, 2, N], F32R)
        hid = sb("hid", [P, 2, CW])
        h_hi = sb("h_hi", [P, NG, 4, H], F32R)
        h_lo = sb("h_lo", [P, NG, 4, H], F32R)
        qT_hi = sb("qT_hi", [P, 2, 2 * N], F32R)
        qT_lo = sb("qT_lo", [P, 2, 2 * N], F32R)
        esum = sb("esum", [P, (NT - 1) * E2 + P])
        esum_tiles = esum[:, 0:NT * E2].rearrange("p (t e) -> p t e", e=E2)
        esumT = sb("esumT", [P, N])
        ones = esumT[:, 0:P]
        junk = sb("junk", [P, D], U8)
        columns = sb("columns", [P, 124])
        taken = [0]

        def cols(*shape):
            n = shape[0] * (shape[1] if len(shape) > 1 else 1)
            part = columns[:, taken[0]:taken[0] + n]
            taken[0] += n
            return part if len(shape) == 1 else part.rearrange("p (a b) -> p a b", b=shape[1])

        gates = cols(3)
        tg = cols(2)
        scale2 = cols(NT)
        c_eps, c_1eps, c_eps2, c_mhalf = cols(NT), cols(NT), cols(NT), cols(E2)
        mean1, var1, rstd1 = cols(NT), cols(NT), cols(2, NT)
        sum2, var2, rstd2 = cols(2, NT), cols(NT), cols(3, NT)
        ssq, ssg, rnorm = cols(NT), cols(NT), cols(2, NT)
        mx, nmax_n = cols(NT, NCH), cols(NT)
        per_slot = cols(3, E2)
        nmax_s, Z_s, rZ_s = (per_slot[:, i, :] for i in range(3))
        Z_n = cols(3, NT)

        ctx_raw = dT[:, :, :, :].rearrange("p a b c -> p (a b c)").rearrange("p (k d) -> p k d", d=D)
        w2_raw = dT[:, :, :, :].rearrange("p a b c -> p (a b c)").rearrange("p (k d) -> p k d", d=D)
        w1_raw = G
        mu_raw = lg
        mu_ss = per_slot
        disp_flat = disp[:, :, :, :].rearrange("p a b c -> p (a b c)")
        ids_raw = disp_flat[:, 0:B * N].bitcast(I32)
        ids_f = disp_flat[:, B * N:2 * B * N]

        bank = [es.enter_context(nc.psum_tensor(f"bank{i}", [P, CW], F32)) for i in range(8)]

        ld_x, ld_ctx, ld_ids, ld_mu, ld_w1, ld_w2, ld_gates, ld_rows = map(
            sem, ("ld_x", "ld_ctx", "ld_ids", "ld_mu", "ld_w1", "ld_w2", "ld_gates", "ld_rows"))
        stored = sem("stored")
        (pl_zero, pl_ident, pl_const, pl_scale, pl_w1, pl_w2, pl_mu_r, pl_rstd1, pl_mask, pl_hb, pl_hlo, pl_rstd2,
         pl_rn) = map(sem, ("pl_zero", "pl_ident", "pl_const", "pl_scale", "pl_w1", "pl_w2", "pl_mu_r", "pl_rstd1",
                            "pl_mask", "pl_hb", "pl_hlo", "pl_rstd2", "pl_rn"))
        (pe_ctxT, pe_mu_ss, pe_mu_bc, pe_hT, pe_u, pe_y, pe_xT, pe_L, pe_T1, pe_T2, pe_G, pe_h, pe_T3, pe_Q, pe_sT,
         pe_out) = map(sem, ("pe_ctxT", "pe_mu_ss", "pe_mu_bc", "pe_hT", "pe_u", "pe_y", "pe_xT", "pe_L", "pe_T1",
                             "pe_T2", "pe_G", "pe_h", "pe_T3", "pe_Q", "pe_sT", "pe_out"))
        (ac_ctx, ac_tg, ac_sq, ac_diag, ac_mu, ac_var1, ac_hT, ac_silu, ac_act, ac_var2, ac_ssq, ac_xT, ac_exp1,
         ac_disp, ac_G, ac_exp2, ac_gelu, ac_h, ac_cT, ac_Q, ac_sT) = map(
            sem, ("ac_ctx", "ac_tg", "ac_sq", "ac_diag", "ac_mu", "ac_var1", "ac_hT", "ac_silu", "ac_act", "ac_var2",
                  "ac_ssq", "ac_xT", "ac_exp1", "ac_disp", "ac_G", "ac_exp2", "ac_gelu", "ac_h", "ac_cT", "ac_Q",
                  "ac_sT"))
        (dv_ids, dv_cls, dv_mask, dv_ctx, dv_mu_ss, dv_mun, dv_mu, dv_mean1, dv_xc1, dv_hn, dv_hT, dv_act, dv_actlo, dv_x1,
         dv_nm2, dv_xc2, dv_xg, dv_xln, dv_ssg, dv_xT, dv_L, dv_M1, dv_M2, dv_disp, dv_rZ, dv_hs, dv_es, dv_Zn,
         dv_cT, dv_Q, dv_fin) = map(
            sem, ("dv_ids", "dv_cls", "dv_mask", "dv_ctx", "dv_mu_ss", "dv_mun", "dv_mu", "dv_mean1", "dv_xc1", "dv_hn",
                  "dv_hT", "dv_act", "dv_actlo", "dv_x1", "dv_nm2", "dv_xc2", "dv_xg", "dv_xln", "dv_ssg", "dv_xT",
                  "dv_L", "dv_M1", "dv_M2", "dv_disp", "dv_rZ", "dv_hs", "dv_es", "dv_Zn", "dv_cT", "dv_Q",
                  "dv_fin"))

        def token_tile(b, nt):
            return x_all[:, bass.ds(b * NT + nt, 1), :].rearrange("p a d -> p (a d)")

        def as_f32(ap):
            return ap.bitcast(F32)

        def used(ring_bank, n=CW):
            return bank[ring_bank][:, 0:n]

        block = es.enter_context(nc.Block())

        @block.sync
        def _(sp):
            for b in range(B):
                sp.dma_start(x_all[:, b * NT:(b + 1) * NT, :],
                             x[b].rearrange("(t p) d -> p t d", p=P)).then_inc(ld_x, 16)
                if b == 0:
                    sp.dma_start(ctx_raw, ctx.rearrange("e (f p) d -> p (e f) d", p=P)).then_inc(ld_ctx, 16)
                    for k in range(DK):
                        sp.dma_start(mu_raw[:, k, :],
                                     mu[k * P:(k + 1) * P].rearrange("p e s -> p (e s)")).then_inc(ld_mu, 16)
            for k in range(DK):
                sp.dma_start(w1_raw[:, k, :].rearrange("p (e h) -> p e h", h=H),
                             W1[:, k * P:(k + 1) * P, :].rearrange("e p h -> p e h")).then_inc(ld_w1, 16)
            sp.wait_ge(pe_ctxT, E)
            sp.dma_start(w2_raw, W2.rearrange("(j two) h d -> (two h) j d", two=2)).then_inc(ld_w2, 16)
            with sp.Fori(0, B) as b:
                sp.wait_ge(dv_fin, nth(b, NT, NT - 1))
                sp.dma_start(out[bass.ds(b, 1)].rearrange("a (t p) d -> p (a t) d", p=P),
                             x_all[:, bass.ds(b * NT, NT), :]).then_inc(stored, 16)
            sp.wait_ge(stored, 16 * B)

        @block.gpsimd
        def _(pool):
            pool.dma_start(gates[:, 0:1], g_xattn.partition_broadcast(P)).then_inc(ld_gates, 16)
            pool.dma_start(gates[:, 1:2], g_ffn.partition_broadcast(P)).then_inc(ld_gates, 16)
            pool.dma_start(gates[:, 2:3], scale.partition_broadcast(P)).then_inc(ld_gates, 16)
            pool.dma_start(ids_raw, ids.rearrange("b n -> (b n)").partition_broadcast(P)).then_inc(ld_ids, 16)
            pool.memset(ident[:, :], 0.0).then_inc(pl_zero, 1)
            for tile, value in ((c_eps, LN_EPS), (c_1eps, 1.0 + LN_EPS), (c_eps2, LN_EPS * LN_EPS),
                                (c_mhalf, -0.5), (ones, 1.0), (esum[:, :], 0.0), (b2_pad[:, :], 0.0)):
                pool.memset(tile, value).then_inc(pl_const, 1)
            pool.wait_ge(pl_zero, 1)
            pool.affine_select(out=ident[:, :], in_=ident[:, :], compare_op=ALU.not_equal, fill=1.0, base=0,
                               pattern=[[-1, P]], channel_multiplier=1).then_inc(pl_ident, 1)
            pool.wait_ge(pl_const, 7)
            pool.dma_start(b2_pad[0:E2, :], b2).then_inc(ld_rows, 16)
            pool.dma_start(gam[:, :], gamma.partition_broadcast(P)).then_inc(ld_rows, 16)
            pool.dma_start(bet[:, :], beta.partition_broadcast(P)).then_inc(ld_rows, 16)
            pool.dma_start(b1_bc[:, :], b1.rearrange("e h -> (e h)").partition_broadcast(P)).then_inc(ld_rows, 16)
            for tile in (h_hi, h_lo):
                pool.memset(as_f32(tile[:, :, :, :]), 0.0).then_inc(pl_const, 1)
            pool.wait_ge(ld_gates, 48)
            for nt in range(NT):
                pool.tensor_copy(scale2[:, nt:nt + 1], gates[:, 2:3]).then_inc(pl_scale, 1)

            def rstd1_step(a):
                pool.wait_ge(ac_var1, nth(a, NT, NT - 1))
                pool.tensor_tensor(rstd1[:, 0, :], var1[:, :], c_eps[:, :], ALU.add).then_inc(pl_rstd1, 1)
                pool.wait_ge(pl_rstd1, nth(a, 2, 0))
                pool.tensor_tensor(rstd1[:, 1, :], rstd1[:, 0, :], c_mhalf[:, 0:NT], ALU.pow).then_inc(pl_rstd1, 1)

            def mask_step(a, e):
                pool.wait_ge(ac_silu, nth(a, E, e))
                pool.wait_ge(dv_mask, nth(a, E, e))
                part = act[:, e % 2, :].rearrange("p (f n) -> p f n", f=2)
                pool.tensor_tensor(part, part, mask[:, e, :].unsqueeze(1).to_broadcast([P, 2, N]),
                                   ALU.mult).then_inc(pl_mask, 1)

            def rstd2_step(a):
                pool.wait_ge(ac_var2, nth(a, NT, NT - 1))
                pool.tensor_tensor(rstd2[:, 0, :], var2[:, :], c_1eps[:, :], ALU.mult).then_inc(pl_rstd2, 1)
                pool.wait_ge(pl_rstd2, nth(a, 3, 0))
                pool.tensor_tensor(rstd2[:, 1, :], rstd2[:, 0, :], c_eps2[:, :], ALU.add).then_inc(pl_rstd2, 1)
                pool.wait_ge(pl_rstd2, nth(a, 3, 1))
                pool.tensor_tensor(rstd2[:, 2, :], rstd2[:, 1, :], c_mhalf[:, 0:NT], ALU.pow).then_inc(pl_rstd2, 1)

            def rnorm_step(a):
                pool.wait_ge(dv_ssg, a + 1)
                pool.tensor_tensor(rnorm[:, 0, :], ssg[:, :], c_mhalf[:, 0:NT], ALU.pow).then_inc(pl_rn, 1)
                pool.wait_ge(pl_rn, nth(a, 2, 0))
                pool.tensor_tensor(rnorm[:, 1, :], rnorm[:, 0, :], scale2[:, :], ALU.mult).then_inc(pl_rn, 1)

            def hidden_bias(b, q):
                pool.wait_ge(dv_hs, nth(b, 2, q))
                part = hid[:, q, :]
                pool.tensor_tensor(part, part, b1_bc[:, q * CW:(q + 1) * CW], ALU.add).then_inc(pl_hb, 1)

            def hidden_lo(b, q):
                pool.wait_ge(ac_h, nth(b, 2, q))
                hi = h_hi[:, 4 * q:4 * q + 4, 0:4:3, :]
                pool.tensor_tensor(h_lo[:, 4 * q:4 * q + 4, 0:4:3, :],
                                   hid[:, q, :].rearrange("p (j t h) -> p j t h", t=2, h=H),
                                   as_f32(hi), ALU.subtract).then_inc(pl_hlo, 1)

            rstd1_step(0)
            pool.wait_ge(ld_w1, 16 * DK)
            for k in range(DK):
                pool.tensor_copy(w1_hi[:, k, :], w1_raw[:, k, :]).then_inc(pl_w1, 1)
            pool.wait_ge(ld_rows, 64)
            for e in range(E):
                mask_step(0, e)
            pool.wait_ge(dv_mu_ss, 3)
            pool.tensor_tensor(mu_ss[:, 2, :], mu_ss[:, 1, :], c_mhalf[:, :], ALU.pow).then_inc(pl_mu_r, 1)
            pool.wait_ge(pl_w1, DK)
            for k in range(DK):
                pool.tensor_tensor(w1_lo[:, k, :], w1_raw[:, k, :], as_f32(w1_hi[:, k, :]),
                                   ALU.subtract).then_inc(pl_w1, 1)
            rstd2_step(0)
            rnorm_step(0)
            pool.wait_ge(ld_w2, 16)
            for j in range(2):
                part = slice(j * NG // 2, (j + 1) * NG // 2)
                pool.tensor_copy(w2_hi[:, part, :], w2_raw[:, part, :]).then_inc(pl_w2, 1)
                pool.wait_ge(pl_w2, 2 * j + 1)
                pool.tensor_tensor(w2_lo[:, part, :], w2_raw[:, part, :], as_f32(w2_hi[:, part, :]),
                                   ALU.subtract).then_inc(pl_w2, 1)

            def iteration(b, a):
                if a is not None:
                    rstd1_step(a)
                for q in range(2):
                    hidden_bias(b, q)
                if a is not None:
                    for e in range(E):
                        mask_step(a, e)
                for q in range(2):
                    hidden_lo(b, q)
                if a is not None:
                    rstd2_step(a)
                    rnorm_step(a)

            iteration(0, 1)
            with pool.Fori(1, B - 1) as b:
                iteration(b, b + 1)
            iteration(B - 1, None)

        @block.scalar
        def _(ac):
            def centred_square(a, var, xc_done, signal):
                for nt in range(NT):
                    ac.wait_ge(xc_done, nth(a, NT, nt))
                    if nt:
                        ac.wait_ge(signal, nth(a, NT, nt - 1))
                    ac.activation(junk[:, :], xc[:, nt, :], ACT.Square, scale=float(D) ** -0.5,
                                  accum_out=var[:, nt:nt + 1]).then_inc(signal, 1)

            def hT_step(a):
                ac.wait_ge(pe_hT, a + 1)
                ac.wait_ge(pe_u, nth(a, E, -1))
                ac.activation(hT_hi[:, :], used(6), ACT.Copy).then_inc(ac_hT, 1)

            def silu_step(a, e):
                ac.wait_ge(pe_u, nth(a, E, e))
                if e >= 2:
                    ac.wait_ge(dv_actlo, nth(a, E, e - 2))
                else:
                    ac.wait_ge(dv_actlo, nth(a, E, -1))
                ac.activation(act[:, e % 2, :], used(e % 2), ACT.Silu).then_inc(ac_silu, 1)

            def act_hi_step(a, e):
                ac.wait_ge(dv_act, nth(a, E, e))
                ac.wait_ge(pe_y, nth(a, E, e - 2) if e >= 2 else nth(a, E, -1))
                ac.activation(act_hi[:, e % 2, :], act[:, e % 2, :], ACT.Copy).then_inc(ac_act, 1)

            def var1_step(a):
                ac.wait_ge(ac_ssq, nth(a, NT, -1))
                centred_square(a, var1, dv_xc1, ac_var1)

            def var2_step(a):
                ac.wait_ge(ac_var1, nth(a, NT, NT - 1))
                centred_square(a, var2, dv_xc2, ac_var2)

            def ssq_step(a):
                ac.wait_ge(ac_var2, nth(a, NT, NT - 1))
                for nt in range(NT):
                    ac.wait_ge(dv_xln, nth(a, NT, nt))
                    if nt:
                        ac.wait_ge(ac_ssq, nth(a, NT, nt - 1))
                    ac.activation(junk[:, :], xc[:, nt, :], ACT.Square,
                                  accum_out=ssq[:, nt:nt + 1]).then_inc(ac_ssq, 1)

            def xT_step(a):
                ac.wait_ge(pe_xT, a + 1)
                ac.activation(xT_hi[:, :], used(5), ACT.Copy).then_inc(ac_xT, 1)

            def exp1(b, g):
                c = g // 2
                ac.wait_ge(dv_M1, nth(b, NG, g))
                ac.wait_ge(pe_T2, nth(b, 2 * NCH, 2 * (c - 2) + 1) if c >= 2 else nth(b, 2 * NCH, -1))
                for j in range(2):
                    s = 2 * g + j
                    last = ac.activation(dT[:, c % 2, s % EPC, :], bank[2 + g % 2][:, j * N:(j + 1) * N], ACT.Exp,
                                         bias=nmax_s[:, s:s + 1], accum_out=Z_s[:, s:s + 1])
                last.then_inc(ac_exp1, 1)

            def disp_step(b, c):
                ac.wait_ge(pe_T2, nth(b, 2 * NCH, 2 * c))
                ac.wait_ge(pe_h, nth(b, NCH, c - 2) if c >= 2 else nth(b, NCH, -1))
                ac.activation(disp[:, c % 2, 0, :], used(4), ACT.Copy).then_inc(ac_disp, 1)

            def G_step(b, k):
                ac.wait_ge(pe_G, nth(b, 4, k))
                ac.wait_ge(pe_h, nth(b, NCH, -1))
                ch, nt = k // 2, k % 2
                ac.activation(G[:, nt, ch * CW:(ch + 1) * CW], used(k % 2), ACT.Copy).then_inc(ac_G, 1)

            def exp2(b, c, nt):
                ac.wait_ge(dv_M2, b + 1)
                ac.wait_ge(pe_T1, nth(b, NG, 2 * c + 1))
                part = lg[:, nt, c * CW:(c + 1) * CW]
                ac.activation(part, part, ACT.Exp, bias=nmax_n[:, nt:nt + 1]).then_inc(ac_exp2, 1)

            def gelu_step(b, q):
                ac.wait_ge(pl_hb, nth(b, 2, q))
                ac.activation(hid[:, q, :], hid[:, q, :], ACT.Gelu).then_inc(ac_gelu, 1)

            def h_hi_step(b, q):
                ac.wait_ge(ac_gelu, nth(b, 2, q))
                ac.wait_ge(pe_Q, nth(b, NCH, -1))
                ac.activation(h_hi[:, 4 * q:4 * q + 4, 0:4:3, :],
                              hid[:, q, :].rearrange("p (j t h) -> p j t h", t=2, h=H), ACT.Copy).then_inc(ac_h, 1)

            def cT_step(b, g):
                ac.wait_ge(pe_T3, nth(b, NG, g))
                ac.wait_ge(pe_Q, nth(b, NCH, g // 2 - 2) if g >= 4 else nth(b, NCH, -1))
                ac.activation(cT_hi[:, g % 4, :, :].rearrange("p j n -> p (j n)"), used(2 + g % 2),
                              ACT.Copy).then_inc(ac_cT, 1)

            def sT_step(b):
                ac.wait_ge(pe_sT, b + 1)
                ac.activation(esumT[:, :], used(4, N), ACT.Copy).then_inc(ac_sT, 1)

            def Q_step(b, c):
                ac.wait_ge(pe_Q, nth(b, NCH, c))
                ac.wait_ge(pe_out, nth(b, NCH, c - 2) if c >= 2 else nth(b, NCH, -1))
                ac.activation(qT_hi[:, c % 2, :], used(c % 2), ACT.Copy).then_inc(ac_Q, 1)

            def sq_step(j):
                c, k = j // DK, j % DK
                ac.wait_ge(ld_mu, 16 * DK)
                if j >= 2:
                    ac.wait_ge(pe_mu_ss, j - 1)
                ac.activation(hid[:, j % 2, :], mu_raw[:, k, c * CW:(c + 1) * CW], ACT.Square).then_inc(ac_sq, 1)

            def mu_hi_step(c, k):
                ac.wait_ge(dv_mun, DK * c + k + 1)
                part = slice(c * CW, (c + 1) * CW)
                ac.activation(mu_hi[:, k, part], mu_raw[:, k, part], ACT.Copy).then_inc(ac_mu, 1)

            ac.wait_ge(ld_gates, 48)
            ac.activation(tg[:, :], gates[:, 0:2], ACT.Tanh).then_inc(ac_tg, 1)
            var1_step(0)
            for e in range(E):
                ac.wait_ge(pe_ctxT, e + 1)
                ac.activation(ctxT_hi[:, :, e * F:(e + 1) * F], used(e).rearrange("p (k f) -> p k f", k=DK),
                              ACT.Copy).then_inc(ac_ctx, 1)
                if e == 1:
                    hT_step(0)
            sq_step(0)
            sq_step(1)
            silu_step(0, 0)
            sq_step(2)
            sq_step(3)
            silu_step(0, 1)
            act_hi_step(0, 0)
            sq_step(4)
            sq_step(5)
            act_hi_step(0, 1)
            silu_step(0, 2)
            sq_step(6)
            sq_step(7)
            act_hi_step(0, 2)
            silu_step(0, 3)
            act_hi_step(0, 3)
            ac.wait_ge(pl_mu_r, 1)
            ac.wait_ge(pe_mu_ss, DK * NCH)
            for c in range(NCH):
                if c >= 2:
                    ac.wait_ge(pe_mu_bc, c - 1)
                for j in range(EPC):
                    s = c * EPC + j
                    last = ac.activation(hid[:, c % 2, j * P:(j + 1) * P], ident[:, :], ACT.Copy,
                                         scale=mu_ss[:, 2, s:s + 1])
                last.then_inc(ac_diag, 1)
                if c == 1:
                    var2_step(0)
                if c >= 1:
                    for k in range(DK):
                        mu_hi_step(c - 1, k)
            for k in range(DK):
                mu_hi_step(NCH - 1, k)
            ssq_step(0)
            xT_step(0)

            def iteration(b, a):
                if a is not None:
                    var1_step(a)
                for g in range(4):
                    exp1(b, g)
                disp_step(b, 0)
                if a is not None:
                    hT_step(a)
                exp1(b, 4)
                exp1(b, 5)
                disp_step(b, 1)
                G_step(b, 0)
                G_step(b, 1)
                exp1(b, 6)
                exp1(b, 7)
                disp_step(b, 2)
                G_step(b, 2)
                G_step(b, 3)
                disp_step(b, 3)
                for c in range(NCH):
                    for nt in range(NT):
                        exp2(b, c, nt)
                if a is not None:
                    silu_step(a, 0)
                    silu_step(a, 1)
                    act_hi_step(a, 0)
                cT_step(b, 0)
                cT_step(b, 1)
                if a is not None:
                    act_hi_step(a, 1)
                    silu_step(a, 2)
                cT_step(b, 2)
                cT_step(b, 3)
                if a is not None:
                    act_hi_step(a, 2)
                    silu_step(a, 3)
                    act_hi_step(a, 3)
                for q in range(2):
                    gelu_step(b, q)
                    h_hi_step(b, q)
                sT_step(b)
                Q_step(b, 0)
                if a is not None:
                    var2_step(a)
                cT_step(b, 4)
                cT_step(b, 5)
                Q_step(b, 1)
                if a is not None:
                    ssq_step(a)
                cT_step(b, 6)
                cT_step(b, 7)
                Q_step(b, 2)
                Q_step(b, 3)
                if a is not None:
                    xT_step(a)

            iteration(0, 1)
            with ac.Fori(1, B - 1) as b:
                iteration(b, b + 1)
            iteration(B - 1, None)

        @block.vector
        def _(dv):
            def split_lo(out_lo, whole, hi):
                return dv.tensor_tensor(out_lo, whole, as_f32(hi), ALU.subtract)

            def centre1(a):
                dv.wait_ge(pe_xT, nth(a, 1, -1))
                dv.wait_ge(ld_x, 16 * B)
                for nt in range(NT):
                    dv.tensor_scalar(xc[:, nt, :], token_tile(a, nt), 1.0 / D, None, ALU.mult, ALU.add,
                                     accum_out=mean1[:, nt:nt + 1]).then_inc(dv_mean1, 1)
                for nt in range(NT):
                    dv.wait_ge(dv_mean1, nth(a, NT, nt))
                    dv.tensor_scalar(xc[:, nt, :], token_tile(a, nt), mean1[:, nt:nt + 1], None,
                                     ALU.subtract).then_inc(dv_xc1, 1)

            def mask_step(a):
                dv.wait_ge(pl_mask, nth(a, E, -1))
                dv.wait_ge(dv_cls, E - 1)
                for e in range(E):
                    dv.tensor_scalar(mask[:, e, :], cls[:, bass.ds(a * N, N)], e, None,
                                     ALU.is_equal).then_inc(dv_mask, 1)

            def norm1(a):
                dv.wait_ge(ac_var1, nth(a, NT, NT - 1))
                dv.wait_ge(pl_rstd1, nth(a, 2, 1))
                for nt in range(NT):
                    dv.tensor_scalar(xc[:, nt, :], xc[:, nt, :], rstd1[:, 1, nt:nt + 1], None,
                                     ALU.mult).then_inc(dv_hn, 1)

            def hT_step(a):
                dv.wait_ge(ac_hT, a + 1)
                split_lo(hT_lo[:, :], used(6), hT_hi[:, :]).then_inc(dv_hT, 1)

            def act_step(a, e):
                dv.wait_ge(pl_mask, nth(a, E, e))
                dv.tensor_tensor(act[:, e % 2, :], used(e % 2), act[:, e % 2, :], ALU.mult).then_inc(dv_act, 1)

            def act_lo_step(a, e):
                dv.wait_ge(ac_act, nth(a, E, e))
                split_lo(act_lo[:, e % 2, :], act[:, e % 2, :], act_hi[:, e % 2, :]).then_inc(dv_actlo, 1)

            def x1_step(a):
                dv.wait_ge(ac_tg, 1)
                dv.wait_ge(pe_y, nth(a, E, E - 1))
                for nt in range(NT):
                    dv.scalar_tensor_tensor(out=token_tile(a, nt), in0=used(6 + nt, D), scalar=tg[:, 0:1],
                                            in1=token_tile(a, nt), op0=ALU.mult, op1=ALU.add,
                                            accum_out=sum2[:, 0, nt:nt + 1]).then_inc(dv_x1, 1)
                dv.wait_ge(dv_x1, nth(a, NT, NT - 1))
                dv.tensor_scalar(sum2[:, 1, :], sum2[:, 0, :], -1.0 / D, None, ALU.mult).then_inc(dv_nm2, 1)
                dv.wait_ge(dv_nm2, a + 1)
                for nt in range(NT):
                    dv.tensor_scalar(xc[:, nt, :], token_tile(a, nt), sum2[:, 1, nt:nt + 1], None,
                                     ALU.add).then_inc(dv_xc2, 1)

            def x_ln_step(a):
                dv.wait_ge(ac_var2, nth(a, NT, NT - 1))
                dv.wait_ge(pl_rstd2, nth(a, 3, 2))
                for nt in range(NT):
                    dv.scalar_tensor_tensor(out=xc[:, nt, :], in0=xc[:, nt, :], scalar=rstd2[:, 2, nt:nt + 1],
                                            in1=gam[:, :], op0=ALU.mult, op1=ALU.mult).then_inc(dv_xg, 1)
                for nt in range(NT):
                    dv.wait_ge(dv_xg, nth(a, NT, nt))
                    dv.tensor_tensor(xc[:, nt, :], xc[:, nt, :], bet[:, :], ALU.add).then_inc(dv_xln, 1)

            def ssg_step(a):
                dv.wait_ge(ac_ssq, nth(a, NT, NT - 1))
                dv.wait_ge(pl_rn, nth(a, 2, -1))
                dv.tensor_scalar(ssg[:, :], ssq[:, :], L2_EPS * L2_EPS, None, ALU.max).then_inc(dv_ssg, 1)

            def xT_step(a):
                dv.wait_ge(ac_xT, a + 1)
                split_lo(xT_lo[:, :], used(5), xT_hi[:, :]).then_inc(dv_xT, 1)

            def logits(b, j):
                c, nt = j // 2, j % 2
                dv.wait_ge(pl_rn, nth(b, 2, 1))
                dv.wait_ge(pe_T3, nth(b, NG, -1))
                dv.wait_ge(dv_es, nth(b, NCH, -1))
                dv.wait_ge(pe_L, nth(b, 2 * NCH, j))
                dv.tensor_scalar(lg[:, nt, c * CW:(c + 1) * CW], used(j % 2), rnorm[:, 1, nt:nt + 1], None,
                                 ALU.mult, ALU.max, accum_out=mx[:, nt, c:c + 1]).then_inc(dv_L, 1)

            def max_s(b, g):
                dv.wait_ge(ac_exp1, nth(b, NG, -1))
                dv.wait_ge(pe_T1, nth(b, NG, g))
                dv.tensor_reduce(nmax_s[:, 2 * g:2 * g + 2], used(2 + g % 2).rearrange("p (j n) -> p j n", j=2),
                                 axis=AX.X, op=ALU.max, negate=True).then_inc(dv_M1, 1)

            def max_n(b):
                dv.wait_ge(dv_L, nth(b, 2 * NCH, 2 * NCH - 1))
                dv.tensor_reduce(nmax_n[:, :], mx[:, :, :], axis=AX.X, op=ALU.max, negate=True).then_inc(dv_M2, 1)

            def disp_step(b, c):
                dv.wait_ge(pe_T2, nth(b, 2 * NCH, 2 * c + 1))
                dv.wait_ge(pe_h, nth(b, NCH, c - 2) if c >= 2 else nth(b, NCH, -1))
                dv.tensor_copy(disp[:, c % 2, 1, :], used(5)).then_inc(dv_disp, 1)

            def rZ_step(b, q):
                dv.wait_ge(ac_exp1, nth(b, NG, 4 * q + 3))
                dv.wait_ge(dv_hs, nth(b, 2, -1))
                half = slice(8 * q, 8 * q + 8)
                dv.reciprocal(rZ_s[:, half], Z_s[:, half]).then_inc(dv_rZ, 1)

            def hidden_scale(b, q):
                dv.wait_ge(dv_rZ, nth(b, 2, q))
                dv.wait_ge(pl_hlo, nth(b, 2, -1))
                dv.wait_ge(pe_h, nth(b, NCH, 2 * q + 1))
                dv.tensor_tensor(hid[:, q, :].rearrange("p (e h) -> p e h", h=H),
                                 used(6 + q).rearrange("p (e h) -> p e h", h=H),
                                 rZ_s[:, 8 * q:8 * q + 8].unsqueeze(2).to_broadcast([P, 8, H]),
                                 ALU.mult).then_inc(dv_hs, 1)

            def esum_step(b, c):
                dv.wait_ge(ac_exp2, nth(b, 2 * NCH, 2 * c + 1))
                dv.wait_ge(pe_sT, nth(b, 1, -1))
                dv.wait_ge(dv_Zn, nth(b, 3, -1))
                dv.tensor_reduce(esum_tiles[:, :, c * EPC:(c + 1) * EPC],
                                 lg[:, :, c * CW:(c + 1) * CW].rearrange("p t (e s) -> p t e s", s=S),
                                 axis=AX.X, op=ALU.add).then_inc(dv_es, 1)

            def Zn_step(b):
                dv.wait_ge(dv_es, nth(b, NCH, NCH - 1))
                dv.wait_ge(dv_fin, nth(b, NT, -1))
                dv.tensor_reduce(Z_n[:, 0, :], esum_tiles, axis=AX.X, op=ALU.add).then_inc(dv_Zn, 1)
                dv.wait_ge(dv_Zn, nth(b, 3, 0))
                dv.reciprocal(Z_n[:, 1, :], Z_n[:, 0, :]).then_inc(dv_Zn, 1)
                dv.wait_ge(dv_Zn, nth(b, 3, 1))
                dv.tensor_scalar(Z_n[:, 2, :], Z_n[:, 1, :], tg[:, 1:2], None, ALU.mult).then_inc(dv_Zn, 1)

            def cT_step(b, g):
                dv.wait_ge(ac_cT, nth(b, NG, g))
                split_lo(cT_lo[:, g % 4, :, :].rearrange("p j n -> p (j n)"), used(2 + g % 2),
                         cT_hi[:, g % 4, :, :].rearrange("p j n -> p (j n)")).then_inc(dv_cT, 1)

            def Q_step(b, c):
                dv.wait_ge(ac_Q, nth(b, NCH, c))
                split_lo(qT_lo[:, c % 2, :], used(c % 2), qT_hi[:, c % 2, :]).then_inc(dv_Q, 1)

            def final(b):
                dv.wait_ge(dv_Zn, nth(b, 3, 2))
                dv.wait_ge(pe_out, nth(b, NCH, NCH - 1))
                for nt in range(NT):
                    dv.scalar_tensor_tensor(out=token_tile(b, nt), in0=used(6 + nt, D), scalar=Z_n[:, 2, nt:nt + 1],
                                            in1=token_tile(b, nt), op0=ALU.mult, op1=ALU.add).then_inc(dv_fin, 1)

            def mu_lo_step(c, k):
                dv.wait_ge(ac_mu, DK * c + k + 1)
                part = slice(c * CW, (c + 1) * CW)
                split_lo(mu_lo[:, k, part], mu_raw[:, k, part], mu_hi[:, k, part]).then_inc(dv_mu, 1)

            centre1(0)
            dv.wait_ge(ld_ids, 16)
            dv.tensor_copy(ids_f, ids_raw).then_inc(dv_ids, 1)
            norm1(0)
            dv.wait_ge(dv_ids, 1)
            for e in range(1, E):
                if e == 1:
                    dv.tensor_scalar(cls[:, :], ids_f, PER_EXPERT, None, ALU.is_ge).then_inc(dv_cls, 1)
                else:
                    dv.wait_ge(dv_cls, e - 1)
                    dv.scalar_tensor_tensor(out=cls[:, :], in0=ids_f, scalar=e * PER_EXPERT, in1=cls[:, :],
                                            op0=ALU.is_ge, op1=ALU.add).then_inc(dv_cls, 1)
            mask_step(0)
            for e in range(E):
                if e == 1:
                    hT_step(0)
                dv.wait_ge(ac_ctx, e + 1)
                part = slice(e * F, (e + 1) * F)
                split_lo(ctxT_lo[:, :, part], used(e).rearrange("p (k f) -> p k f", k=DK),
                         ctxT_hi[:, :, part]).then_inc(dv_ctx, 1)
            act_step(0, 0)
            act_lo_step(0, 0)
            act_step(0, 1)
            act_lo_step(0, 1)
            act_step(0, 2)
            act_lo_step(0, 2)
            act_step(0, 3)
            act_lo_step(0, 3)
            dv.wait_ge(pe_mu_ss, DK * NCH)
            dv.tensor_copy(mu_ss[:, 0, :], bank[5][:, 0:E2]).then_inc(dv_mu_ss, 1)
            dv.wait_ge(dv_mu_ss, 1)
            dv.tensor_tensor(mu_ss[:, 0, :], bank[5][:, E2:2 * E2], mu_ss[:, 0, :], ALU.add).then_inc(dv_mu_ss, 1)
            dv.wait_ge(dv_mu_ss, 2)
            dv.tensor_scalar(mu_ss[:, 1, :], mu_ss[:, 0, :], L2_EPS * L2_EPS, None, ALU.max).then_inc(dv_mu_ss, 1)
            x1_step(0)
            for c in range(NCH):
                dv.wait_ge(pe_mu_bc, c + 1)
                for k in range(DK):
                    part = mu_raw[:, k, c * CW:(c + 1) * CW]
                    dv.tensor_tensor(part, used(2 + c % 2), part, ALU.mult).then_inc(dv_mun, 1)
                if c == 0:
                    x_ln_step(0)
                if c >= 1:
                    for k in range(DK):
                        mu_lo_step(c - 1, k)
            for k in range(DK):
                mu_lo_step(NCH - 1, k)
            ssg_step(0)
            xT_step(0)

            def iteration(b, a):
                if a is not None:
                    centre1(a)
                logits(b, 0)
                logits(b, 1)
                if a is not None:
                    norm1(a)
                logits(b, 2)
                logits(b, 3)
                max_s(b, 0)
                max_s(b, 1)
                logits(b, 4)
                logits(b, 5)
                max_s(b, 2)
                max_s(b, 3)
                disp_step(b, 0)
                if a is not None:
                    hT_step(a)
                logits(b, 6)
                logits(b, 7)
                max_s(b, 4)
                max_s(b, 5)
                max_n(b)
                disp_step(b, 1)
                rZ_step(b, 0)
                max_s(b, 6)
                max_s(b, 7)
                disp_step(b, 2)
                hidden_scale(b, 0)
                disp_step(b, 3)
                rZ_step(b, 1)
                esum_step(b, 0)
                hidden_scale(b, 1)
                if a is not None:
                    mask_step(a)
                for c in range(1, NCH):
                    esum_step(b, c)
                if a is not None:
                    act_step(a, 0)
                    act_lo_step(a, 0)
                cT_step(b, 0)
                cT_step(b, 1)
                if a is not None:
                    act_step(a, 1)
                    act_lo_step(a, 1)
                    act_step(a, 2)
                cT_step(b, 2)
                cT_step(b, 3)
                if a is not None:
                    act_lo_step(a, 2)
                    act_step(a, 3)
                    act_lo_step(a, 3)
                    x1_step(a)
                Zn_step(b)
                Q_step(b, 0)
                cT_step(b, 4)
                cT_step(b, 5)
                if a is not None:
                    x_ln_step(a)
                Q_step(b, 1)
                cT_step(b, 6)
                cT_step(b, 7)
                if a is not None:
                    ssg_step(a)
                Q_step(b, 2)
                Q_step(b, 3)
                if a is not None:
                    xT_step(a)
                final(b)

            iteration(0, 1)
            with dv.Fori(1, B - 1) as b:
                iteration(b, b + 1)
            iteration(B - 1, None)

        @block.tensor
        def _(pe):
            def mm(out_ap, lhsT, rhs, start, stop):
                return pe.matmul(out_ap, lhsT, rhs, start=start, stop=stop, skip_group_check=True)

            def mm_split(out_ap, lhs, rhs, start, stop):
                mm(out_ap, lhs[0], rhs[0], start, False)
                mm(out_ap, lhs[0], rhs[1], False, False)
                return mm(out_ap, lhs[1], rhs[0], False, stop)

            def hT_transposes(a):
                pe.wait_ge(pl_ident, 1)
                for nt in range(NT):
                    pe.wait_ge(dv_hn, nth(a, NT, nt))
                    for k in range(DK):
                        last = pe.transpose(bank[6][:, k * N + nt * P:k * N + (nt + 1) * P],
                                            xc[:, nt, k * P:(k + 1) * P], ident[:, :])
                last.then_inc(pe_hT, 1)

            def u_step(a, e):
                if e == 0:
                    pe.wait_ge(ac_hT, a + 1)
                    pe.wait_ge(dv_hT, a + 1)
                if e >= 2:
                    pe.wait_ge(dv_act, nth(a, E, e - 2))
                for f in range(2):
                    for k in range(DK):
                        cols = slice(e * F + f * P, e * F + (f + 1) * P)
                        rows = slice(k * N, (k + 1) * N)
                        last = mm_split(bank[e % 2][:, f * N:(f + 1) * N],
                                        (ctxT_hi[:, k, cols], ctxT_lo[:, k, cols]),
                                        (hT_hi[:, rows], hT_lo[:, rows]), k == 0, k == DK - 1)
                last.then_inc(pe_u, 1)

            def y_step(a, e):
                pe.wait_ge(ac_act, nth(a, E, e))
                pe.wait_ge(dv_actlo, nth(a, E, e))
                for nt in range(NT):
                    for f in range(2):
                        tok = slice(f * N + nt * P, f * N + (nt + 1) * P)
                        cols = slice(e * F, (e + 1) * F)
                        last = mm_split(used(6 + nt, D), (act_hi[:, e % 2, tok], act_lo[:, e % 2, tok]),
                                        (ctxT_hi[:, f, cols], ctxT_lo[:, f, cols]),
                                        e == 0 and f == 0, e == E - 1 and f == 1)
                last.then_inc(pe_y, 1)

            def xT_transposes(a):
                for nt in range(NT):
                    pe.wait_ge(dv_xln, nth(a, NT, nt))
                    for k in range(DK):
                        last = pe.transpose(bank[5][:, k * N + nt * P:k * N + (nt + 1) * P],
                                            xc[:, nt, k * P:(k + 1) * P], ident[:, :])
                last.then_inc(pe_xT, 1)

            def x_rows(k, nt):
                rows = slice(k * N + nt * P, k * N + (nt + 1) * P)
                return xT_hi[:, rows], xT_lo[:, rows]

            def L_step(b, j):
                c, nt = j // 2, j % 2
                cols = slice(c * CW, (c + 1) * CW)
                if j < 2:
                    pe.wait_ge(ac_xT, b + 1)
                    pe.wait_ge(dv_xT, b + 1)
                    pe.wait_ge(dv_Q, nth(b, NCH, -1))
                else:
                    pe.wait_ge(dv_L, nth(b, 2 * NCH, j - 2))
                for k in range(DK):
                    last = mm_split(used(j % 2), x_rows(k, nt), (mu_hi[:, k, cols], mu_lo[:, k, cols]),
                                    k == 0, k == DK - 1)
                last.then_inc(pe_L, 1)

            def G_step(b, i):
                ch, nt = i // 2, i % 2
                cols = slice(ch * CW, (ch + 1) * CW)
                if i < 2:
                    pe.wait_ge(dv_L, nth(b, 2 * NCH, 6 + i))
                else:
                    pe.wait_ge(ac_G, nth(b, 4, i - 2))
                for k in range(DK):
                    last = mm_split(used(i % 2), x_rows(k, nt), (w1_hi[:, k, cols], w1_lo[:, k, cols]),
                                    k == 0, k == DK - 1)
                last.then_inc(pe_G, 1)

            def T1_step(b, g):
                c = g // 2
                pe.wait_ge(dv_L, nth(b, 2 * NCH, 2 * c + 1))
                if g >= 2:
                    pe.wait_ge(ac_exp1, nth(b, NG, g - 2))
                else:
                    pe.wait_ge(dv_cT, nth(b, NG, -1))
                for j in range(2):
                    for nt in range(NT):
                        s = (2 * g + j) * S
                        last = pe.transpose(bank[2 + g % 2][:, j * N + nt * P:j * N + (nt + 1) * P],
                                            lg[:, nt, s:s + S], ident[:, :])
                last.then_inc(pe_T1, 1)

            def T2_step(b, c):
                pe.wait_ge(ac_exp1, nth(b, NG, 2 * c + 1))
                for nt in range(NT):
                    if nt == 0:
                        pe.wait_ge(ac_sT, nth(b, 1, -1))
                        if c:
                            pe.wait_ge(ac_disp, nth(b, NCH, c - 1))
                    elif c:
                        pe.wait_ge(dv_disp, nth(b, NCH, c - 1))
                    for j in range(EPC):
                        last = pe.transpose(bank[4 + nt][:, j * S:(j + 1) * S],
                                            dT[:, c % 2, j, nt * P:(nt + 1) * P], ident[:, :])
                    last.then_inc(pe_T2, 1)

            def h_step(b, c):
                pe.wait_ge(ac_disp, nth(b, NCH, c))
                pe.wait_ge(dv_disp, nth(b, NCH, c))
                pe.wait_ge(ac_G, nth(b, 4, 2 * (c // 2) + 1))
                pe.wait_ge(dv_fin, nth(b, NT, -1))
                for j in range(EPC):
                    e = c * EPC + j
                    for nt in range(NT):
                        last = mm(bank[6 + c // 2][:, (e % 8) * H:(e % 8 + 1) * H],
                                  disp[:, c % 2, nt, j * S:(j + 1) * S], G[:, nt, e * H:(e + 1) * H],
                                  nt == 0, nt == NT - 1)
                last.then_inc(pe_h, 1)

            def T3_step(b, g):
                pe.wait_ge(ac_exp2, nth(b, 2 * NCH, 2 * (g // 2) + 1))
                if g >= 2:
                    pe.wait_ge(dv_cT, nth(b, NG, g - 2))
                else:
                    pe.wait_ge(ac_exp1, nth(b, NG, 6 + g))
                for j in range(2):
                    for nt in range(NT):
                        s = (2 * g + j) * S
                        last = pe.transpose(bank[2 + g % 2][:, j * N + nt * P:j * N + (nt + 1) * P],
                                            lg[:, nt, s:s + S], ident[:, :])
                last.then_inc(pe_T3, 1)

            def Q_step(b, c):
                pe.wait_ge(ac_h, nth(b, 2, c // 2))
                pe.wait_ge(pl_hlo, nth(b, 2, c // 2))
                pe.wait_ge(dv_cT, nth(b, NG, 2 * c + 1))
                if c >= 2:
                    pe.wait_ge(dv_Q, nth(b, NCH, c - 2))
                for i in range(2):
                    p = 2 * c + i
                    for t in range(2):
                        lhs = [w[:, p, 2 * t:2 * t + 2, :].rearrange("p a h -> p (a h)") for w in (h_hi, h_lo)]
                        last = mm_split(bank[c % 2][:, i * N:(i + 1) * N], lhs,
                                        (cT_hi[:, p % 4, t, :], cT_lo[:, p % 4, t, :]), t == 0, t == 1)
                last.then_inc(pe_Q, 1)

            def sT_transposes(b):
                pe.wait_ge(dv_es, nth(b, NCH, NCH - 1))
                pe.wait_ge(ac_disp, nth(b, NCH, NCH - 1))
                for nt in range(NT):
                    last = pe.transpose(bank[4][:, nt * P:(nt + 1) * P], esum[:, nt * E2:nt * E2 + P], ident[:, :])
                last.then_inc(pe_sT, 1)

            def out_step(b, c):
                if c == 0:
                    pe.wait_ge(ac_sT, b + 1)
                    for nt in range(NT):
                        mm(used(6 + nt, D), esumT[:, nt * P:(nt + 1) * P], b2_pad[:, :], True, False)
                pe.wait_ge(ac_Q, nth(b, NCH, c))
                pe.wait_ge(dv_Q, nth(b, NCH, c))
                for i in range(2):
                    p = 2 * c + i
                    for nt in range(NT):
                        rows = slice(i * N + nt * P, i * N + (nt + 1) * P)
                        last = mm_split(used(6 + nt, D), (qT_hi[:, c % 2, rows], qT_lo[:, c % 2, rows]),
                                        (w2_hi[:, p, :], w2_lo[:, p, :]), False, p == NG - 1)
                last.then_inc(pe_out, 1)

            pe.wait_ge(pl_ident, 1)
            pe.wait_ge(ld_ctx, 16)
            for e in range(E):
                for f in range(2):
                    for k in range(DK):
                        last = pe.transpose(bank[e][:, k * F + f * P:k * F + (f + 1) * P],
                                            ctx_raw[:, e * 2 + f, k * P:(k + 1) * P], ident[:, :])
                last.then_inc(pe_ctxT, 1)
                if e == 1:
                    hT_transposes(0)

            def mu_squares(c):
                for k in range(DK):
                    pe.wait_ge(ac_sq, DK * c + k + 1)
                    for j in range(EPC):
                        s = k * E2 + c * EPC + j
                        last = mm(bank[5][:, s:s + 1], hid[:, k, j * P:(j + 1) * P], ones[:, 0:1], True, True)
                    last.then_inc(pe_mu_ss, 1)

            pe.wait_ge(pl_const, 7)
            pe.wait_ge(ac_ctx, E)
            pe.wait_ge(dv_ctx, E)
            u_step(0, 0)
            mu_squares(0)
            u_step(0, 1)
            mu_squares(1)
            y_step(0, 0)
            u_step(0, 2)
            mu_squares(2)
            y_step(0, 1)
            u_step(0, 3)
            mu_squares(3)
            y_step(0, 2)
            y_step(0, 3)
            for c in range(NCH):
                pe.wait_ge(ac_diag, c + 1)
                if c >= 2:
                    pe.wait_ge(dv_mun, DK * (c - 1))
                mm(used(2 + c % 2), ones[:, :], hid[:, c % 2, :], True, True).then_inc(pe_mu_bc, 1)
            xT_transposes(0)
            pe.wait_ge(ac_mu, DK * NCH)
            pe.wait_ge(dv_mu, DK * NCH)
            pe.wait_ge(pl_w1, 2 * DK)
            pe.wait_ge(pl_w2, 4)
            pe.wait_ge(ld_rows, 64)

            def iteration(b, a):
                for j in range(4):
                    L_step(b, j)
                T1_step(b, 0)
                T1_step(b, 1)
                L_step(b, 4)
                L_step(b, 5)
                T1_step(b, 2)
                T1_step(b, 3)
                T2_step(b, 0)
                if a is not None:
                    hT_transposes(a)
                L_step(b, 6)
                L_step(b, 7)
                T1_step(b, 4)
                T1_step(b, 5)
                T2_step(b, 1)
                G_step(b, 0)
                G_step(b, 1)
                T1_step(b, 6)
                T1_step(b, 7)
                if a is not None:
                    pe.wait_ge(dv_hT, a + 1)
                h_step(b, 0)
                T2_step(b, 2)
                G_step(b, 2)
                G_step(b, 3)
                h_step(b, 1)
                T2_step(b, 3)
                h_step(b, 2)
                h_step(b, 3)
                pe.wait_ge(ac_G, nth(b, 4, 3))
                if a is not None:
                    u_step(a, 0)
                    u_step(a, 1)
                T3_step(b, 0)
                T3_step(b, 1)
                pe.wait_ge(dv_hs, nth(b, 2, 1))
                if a is not None:
                    y_step(a, 0)
                    u_step(a, 2)
                T3_step(b, 2)
                T3_step(b, 3)
                if a is not None:
                    y_step(a, 1)
                    u_step(a, 3)
                    y_step(a, 2)
                    y_step(a, 3)
                sT_transposes(b)
                if a is not None:
                    pe.wait_ge(dv_act, nth(a, E, 3))
                Q_step(b, 0)
                T3_step(b, 4)
                T3_step(b, 5)
                Q_step(b, 1)
                if a is not None:
                    pe.wait_ge(dv_x1, nth(a, NT, NT - 1))
                out_step(b, 0)
                T3_step(b, 6)
                T3_step(b, 7)
                Q_step(b, 2)
                out_step(b, 1)
                Q_step(b, 3)
                out_step(b, 2)
                if a is not None:
                    pe.wait_ge(dv_disp, nth(b, NCH, NCH - 1))
                    xT_transposes(a)
                out_step(b, 3)

            iteration(0, 1)
            with pe.Fori(1, B - 1) as b:
                iteration(b, b + 1)
            iteration(B - 1, None)


_INS = ["x", "itok_BxS_13_99985", "ctx_2048", "g_xattn", "g_ffn", "L0_ffn_gamma", "L0_ffn_beta", "L0_ffn_mu",
        "L0_ffn_scale", "L0_ffn_W1", "L0_ffn_b1", "L0_ffn_W2", "L0_ffn_b2"]


def kernel(**inputs):
    import numpy as np
    import concourse.bacc as bacc
    from concourse.bass_utils import run_bass_kernel_spmd

    nc = bacc.Bacc("TRN2", target_bir_lowering=False, num_devices=1)
    arrays, args = {}, []
    for name in _INS:
        a = np.ascontiguousarray(inputs[name])
        arrays[f"in_{name}"] = a
        args.append(nc.dram_tensor(f"in_{name}", a.shape, mybir.dt.from_np(a.dtype), kind="ExternalInput").ap())
    out = nc.dram_tensor("out_x", inputs["x"].shape, F32, kind="ExternalOutput").ap()
    flamingo_kernel(nc, *args, out)
    r = run_bass_kernel_spmd(nc, [arrays], core_ids=[0])
    return r.results[0]["out_x"]
```

```python
from contextlib import ExitStack

import concourse.bass as bass
from concourse import mybir

F32 = mybir.dt.float32
F32R = mybir.dt.float32r
I32 = mybir.dt.int32
U8 = mybir.dt.uint8
BF16 = mybir.dt.bfloat16
ALU = mybir.AluOpType
ACT = mybir.ActivationFunctionType
AX = mybir.AxisListType

P = 128
VOCAB = 12500
LN_EPS = 1e-5
L2_EPS = 1e-12


def is_first(b):
    return isinstance(b, int) and b == 0


def nth(b, per_batch, j):
    return b * per_batch + (j + 1)


def flamingo_kernel(nc, x, ids, ctx, g_xattn, g_ffn, gamma, beta, mu, scale, W1, b1, W2, b2, out):
    B, N, D = x.shape
    E, F, _ = ctx.shape
    _, E2, S = mu.shape
    H = W1.shape[2]
    NT = N // P
    DK = D // P
    ES = E2 * S
    EH = E2 * H
    CW = 512
    NCH = ES // CW
    EPC = CW // S
    NG = E2 // 2
    PER_EXPERT = VOCAB // E
    assert (NT, DK, S, 2 * H, F, E, EPC) == (2, 2, P, P, D, 4, 4)

    es = ExitStack()
    with es:
        def sb(name, shape, dt=F32):
            return es.enter_context(nc.sbuf_tensor(name, shape, dt))

        def sem(name):
            return es.enter_context(nc.semaphore(name))

        x_all = sb("x_all", [P, B * NT, D])
        xc = sb("xc", [P, NT, D])
        hT_hi = sb("hT_hi", [P, DK * N], F32R)
        hT_lo = sb("hT_lo", [P, DK * N], F32R)
        ctxT_hi = sb("ctxT_hi", [P, DK, E * F], F32R)
        ctxT_lo = sb("ctxT_lo", [P, DK, E * F], F32R)
        act = sb("act", [P, 2, 2 * N])
        act_hi = sb("act_hi", [P, 2, 2 * N], F32R)
        act_lo = sb("act_lo", [P, 2, 2 * N], F32R)
        cls = sb("cls", [P, B * N], U8)
        mask = sb("mask", [P, E, N], BF16)
        xT_hi = sb("xT_hi", [P, DK * N], F32R)
        xT_lo = sb("xT_lo", [P, DK * N], F32R)
        mu_hi = sb("mu_hi", [P, DK, ES], F32R)
        mu_lo = sb("mu_lo", [P, DK, ES], F32R)
        w1_hi = sb("w1_hi", [P, DK, EH], F32R)
        w1_lo = sb("w1_lo", [P, DK, EH], F32R)
        w2_hi = sb("w2_hi", [P, NG, D], F32R)
        w2_lo = sb("w2_lo", [P, NG, D], F32R)
        b1_bc = sb("b1_bc", [P, EH])
        b2_pad = sb("b2_pad", [P, D])
        gam = sb("gam", [P, D])
        bet = sb("bet", [P, D])
        ident = sb("ident", [P, P])
        G = sb("G", [P, NT, EH])
        lg = sb("lg", [P, NT, ES])
        dT = sb("dT", [P, 2, EPC, N])
        disp = sb("disp", [P, 2, NT, CW])
        cT_hi = sb("cT_hi", [P, 4, 2, N], F32R)
        cT_lo = sb("cT_lo", [P, 4, 2, N], F32R)
        hid = sb("hid", [P, 2, CW])
        h_hi = sb("h_hi", [P, NG, 4, H], F32R)
        h_lo = sb("h_lo", [P, NG, 4, H], F32R)
        qT_hi = sb("qT_hi", [P, 2, 2 * N], F32R)
        qT_lo = sb("qT_lo", [P, 2, 2 * N], F32R)
        esum = sb("esum", [P, (NT - 1) * E2 + P])
        esum_tiles = esum[:, 0:NT * E2].rearrange("p (t e) -> p t e", e=E2)
        esumT = sb("esumT", [P, N])
        ones = esumT[:, 0:P]
        junk = sb("junk", [P, D], U8)
        columns = sb("columns", [P, 124])
        taken = [0]

        def cols(*shape):
            n = shape[0] * (shape[1] if len(shape) > 1 else 1)
            part = columns[:, taken[0]:taken[0] + n]
            taken[0] += n
            return part if len(shape) == 1 else part.rearrange("p (a b) -> p a b", b=shape[1])

        gates = cols(3)
        tg = cols(2)
        scale2 = cols(NT)
        c_eps, c_1eps, c_eps2, c_mhalf = cols(NT), cols(NT), cols(NT), cols(E2)
        mean1, var1, rstd1 = cols(NT), cols(NT), cols(2, NT)
        sum2, var2, rstd2 = cols(2, NT), cols(NT), cols(3, NT)
        ssq, ssg, rnorm = cols(NT), cols(NT), cols(2, NT)
        mx, nmax_n = cols(NT, NCH), cols(NT)
        per_slot = cols(3, E2)
        nmax_s, Z_s, rZ_s = (per_slot[:, i, :] for i in range(3))
        Z_n = cols(3, NT)

        ctx_raw = dT[:, :, :, :].rearrange("p a b c -> p (a b c)").rearrange("p (k d) -> p k d", d=D)
        w2_raw = dT[:, :, :, :].rearrange("p a b c -> p (a b c)").rearrange("p (k d) -> p k d", d=D)
        w1_raw = G
        mu_raw = lg
        mu_ss = per_slot
        disp_flat = disp[:, :, :, :].rearrange("p a b c -> p (a b c)")
        ids_raw = disp_flat[:, 0:B * N].bitcast(I32)
        ids_f = disp_flat[:, B * N:2 * B * N]

        bank = [es.enter_context(nc.psum_tensor(f"bank{i}", [P, CW], F32)) for i in range(8)]

        U_BANK = (0, 1, 4, 5)

        ld_x0, ld_x, ld_ids, ld_mu, ld_w1, ld_w2, ld_gates, ld_rows = map(
            sem, ("ld_x0", "ld_x", "ld_ids", "ld_mu", "ld_w1", "ld_w2", "ld_gates", "ld_rows"))
        ld_ctx = [sem(f"ld_ctx{e}") for e in range(E)]
        stored = sem("stored")
        (pl_zero, pl_ident, pl_const, pl_scale, pl_w1, pl_w2, pl_mu_r, pl_rstd1, pl_mask, pl_hb, pl_hzero, pl_rstd2,
         pl_rn) = map(sem, ("pl_zero", "pl_ident", "pl_const", "pl_scale", "pl_w1", "pl_w2", "pl_mu_r", "pl_rstd1",
                            "pl_mask", "pl_hb", "pl_hzero", "pl_rstd2", "pl_rn"))
        (pe_ctxT, pe_mu_ss, pe_mu_bc, pe_hT, pe_u, pe_y, pe_xT, pe_L, pe_T1, pe_T2, pe_G, pe_h, pe_T3, pe_Q, pe_sT,
         pe_out) = map(sem, ("pe_ctxT", "pe_mu_ss", "pe_mu_bc", "pe_hT", "pe_u", "pe_y", "pe_xT", "pe_L", "pe_T1",
                             "pe_T2", "pe_G", "pe_h", "pe_T3", "pe_Q", "pe_sT", "pe_out"))
        (ac_w1, ac_w2, ac_ctx, ac_tg, ac_sq, ac_diag, ac_mu, ac_var1, ac_hT, ac_silu, ac_act, ac_var2, ac_ssq, ac_xT, ac_exp1,
         ac_disp, ac_G, ac_exp2, ac_gelu, ac_h, ac_cT, ac_Q, ac_sT) = map(
            sem, ("ac_w1", "ac_w2", "ac_ctx", "ac_tg", "ac_sq", "ac_diag", "ac_mu", "ac_var1", "ac_hT", "ac_silu", "ac_act", "ac_var2",
                  "ac_ssq", "ac_xT", "ac_exp1", "ac_disp", "ac_G", "ac_exp2", "ac_gelu", "ac_h", "ac_cT", "ac_Q",
                  "ac_sT"))
        (dv_ids, dv_cls, dv_mask, dv_ctx, dv_mu_ss, dv_mun, dv_mu, dv_mean1, dv_xc1, dv_hn, dv_hT, dv_act, dv_actlo, dv_x1,
         dv_nm2, dv_xc2, dv_xg, dv_xln, dv_ssg, dv_xT, dv_L, dv_M1, dv_M2, dv_disp, dv_rZ, dv_hs, dv_es, dv_Zn,
         dv_hlo, dv_cT, dv_Q, dv_fin) = map(
            sem, ("dv_ids", "dv_cls", "dv_mask", "dv_ctx", "dv_mu_ss", "dv_mun", "dv_mu", "dv_mean1", "dv_xc1", "dv_hn",
                  "dv_hT", "dv_act", "dv_actlo", "dv_x1", "dv_nm2", "dv_xc2", "dv_xg", "dv_xln", "dv_ssg", "dv_xT",
                  "dv_L", "dv_M1", "dv_M2", "dv_disp", "dv_rZ", "dv_hs", "dv_es", "dv_Zn", "dv_hlo", "dv_cT", "dv_Q",
                  "dv_fin"))

        def token_tile(b, nt):
            return x_all[:, bass.ds(b * NT + nt, 1), :].rearrange("p a d -> p (a d)")

        def as_f32(ap):
            return ap.bitcast(F32)

        def used(ring_bank, n=CW):
            return bank[ring_bank][:, 0:n]

        block = es.enter_context(nc.Block())

        @block.sync
        def _(sp):
            def load_x(b, done):
                sp.dma_start(x_all[:, b * NT:(b + 1) * NT, :],
                             x[b].rearrange("(t p) d -> p t d", p=P)).then_inc(done, 16)

            load_x(0, ld_x0)
            for e in range(E):
                sp.dma_start(ctx_raw[:, 2 * e:2 * e + 2, :], ctx[e].rearrange("(f p) d -> p f d", p=P)).then_inc(ld_ctx[e], 16)
            for k in range(DK):
                sp.dma_start(mu_raw[:, k, :], mu[k * P:(k + 1) * P].rearrange("p e s -> p (e s)")).then_inc(ld_mu, 16)
            for k in range(DK):
                sp.dma_start(w1_raw[:, k, :].rearrange("p (e h) -> p e h", h=H),
                             W1[:, k * P:(k + 1) * P, :].rearrange("e p h -> p e h")).then_inc(ld_w1, 16)
            sp.wait_ge(pe_ctxT, E)
            sp.dma_start(w2_raw, W2.rearrange("(j two) h d -> (two h) j d", two=2)).then_inc(ld_w2, 16)
            for b in range(1, B):
                load_x(b, ld_x)
            sp.wait_ge(pl_const, 7)
            sp.dma_start(b2_pad[0:E2, :], b2).then_inc(ld_rows, 16)
            with sp.Fori(0, B) as b:
                sp.wait_ge(dv_fin, nth(b, NT, NT - 1))
                sp.dma_start(out[bass.ds(b, 1)].rearrange("a (t p) d -> p (a t) d", p=P),
                             x_all[:, bass.ds(b * NT, NT), :]).then_inc(stored, 16)
            sp.wait_ge(stored, 16 * B)

        @block.gpsimd
        def _(pool):
            pool.memset(ident[:, :], 0.0).then_inc(pl_zero, 1)
            pool.wait_ge(pl_zero, 1)
            pool.affine_select(out=ident[:, :], in_=ident[:, :], compare_op=ALU.not_equal, fill=1.0, base=0,
                               pattern=[[-1, P]], channel_multiplier=1).then_inc(pl_ident, 1)
            for tile, value in ((c_eps, LN_EPS), (c_1eps, 1.0 + LN_EPS), (c_eps2, LN_EPS * LN_EPS),
                                (c_mhalf, -0.5), (ones, 1.0), (esum[:, :], 0.0), (b2_pad[:, :], 0.0)):
                pool.memset(tile, value).then_inc(pl_const, 1)
            pool.wait_ge(pl_const, 7)
            pool.wait_ge(ld_gates, 48)
            for nt in range(NT):
                pool.tensor_copy(scale2[:, nt:nt + 1], gates[:, 2:3]).then_inc(pl_scale, 1)

            def rstd1_step(a):
                pool.wait_ge(ac_var1, nth(a, NT, NT - 1))
                pool.tensor_tensor(rstd1[:, 0, :], var1[:, :], c_eps[:, :], ALU.add).then_inc(pl_rstd1, 1)
                pool.wait_ge(pl_rstd1, nth(a, 2, 0))
                pool.tensor_tensor(rstd1[:, 1, :], rstd1[:, 0, :], c_mhalf[:, 0:NT], ALU.pow).then_inc(pl_rstd1, 1)

            def mask_step(a, e):
                pool.wait_ge(ac_silu, nth(a, E, e))
                pool.wait_ge(dv_mask, nth(a, E, e))
                part = act[:, e % 2, :].rearrange("p (f n) -> p f n", f=2)
                pool.tensor_tensor(part, part, mask[:, e, :].unsqueeze(1).to_broadcast([P, 2, N]),
                                   ALU.mult).then_inc(pl_mask, 1)

            def rstd2_step(a):
                pool.wait_ge(ac_var2, nth(a, NT, NT - 1))
                pool.tensor_tensor(rstd2[:, 0, :], var2[:, :], c_1eps[:, :], ALU.mult).then_inc(pl_rstd2, 1)
                pool.wait_ge(pl_rstd2, nth(a, 3, 0))
                pool.tensor_tensor(rstd2[:, 1, :], rstd2[:, 0, :], c_eps2[:, :], ALU.add).then_inc(pl_rstd2, 1)
                pool.wait_ge(pl_rstd2, nth(a, 3, 1))
                pool.tensor_tensor(rstd2[:, 2, :], rstd2[:, 1, :], c_mhalf[:, 0:NT], ALU.pow).then_inc(pl_rstd2, 1)

            def rnorm_step(a):
                pool.wait_ge(dv_ssg, a + 1)
                pool.tensor_tensor(rnorm[:, 0, :], ssg[:, :], c_mhalf[:, 0:NT], ALU.pow).then_inc(pl_rn, 1)
                pool.wait_ge(pl_rn, nth(a, 2, 0))
                if is_first(a):
                    pool.wait_ge(pl_scale, NT)
                pool.tensor_tensor(rnorm[:, 1, :], rnorm[:, 0, :], scale2[:, :], ALU.mult).then_inc(pl_rn, 1)

            def hidden_bias(b, q):
                pool.wait_ge(dv_hs, nth(b, 2, q))
                part = hid[:, q, :]
                pool.tensor_tensor(part, part, b1_bc[:, q * CW:(q + 1) * CW], ALU.add).then_inc(pl_hb, 1)

            rstd1_step(0)
            for tile in (h_hi, h_lo):
                pool.memset(as_f32(tile[:, :, :, :]), 0.0).then_inc(pl_hzero, 1)
            mask_step(0, 0)
            mask_step(0, 1)
            pool.wait_ge(dv_mu_ss, 3)
            pool.tensor_tensor(mu_ss[:, 2, :], mu_ss[:, 1, :], c_mhalf[:, :], ALU.pow).then_inc(pl_mu_r, 1)
            mask_step(0, 2)
            mask_step(0, 3)
            rstd2_step(0)
            for k in range(DK):
                pool.wait_ge(ac_w1, k + 1)
                pool.tensor_tensor(w1_lo[:, k, :], w1_raw[:, k, :], as_f32(w1_hi[:, k, :]),
                                   ALU.subtract).then_inc(pl_w1, 1)
            rnorm_step(0)
            for j in range(2):
                pool.wait_ge(ac_w2, j + 1)
                part = slice(j * NG // 2, (j + 1) * NG // 2)
                pool.tensor_tensor(w2_lo[:, part, :], w2_raw[:, part, :], as_f32(w2_hi[:, part, :]),
                                   ALU.subtract).then_inc(pl_w2, 1)
            pool.wait_ge(ld_rows, 64)

            def iteration(b, a):
                if a is not None:
                    rstd1_step(a)
                hidden_bias(b, 0)
                if a is not None:
                    mask_step(a, 0)
                hidden_bias(b, 1)
                if a is not None:
                    for e in range(1, E):
                        mask_step(a, e)
                    rstd2_step(a)
                    rnorm_step(a)

            iteration(0, 1)
            with pool.Fori(1, B - 1) as b:
                iteration(b, b + 1)
            iteration(B - 1, None)

        @block.scalar
        def _(ac):
            def centred_square(a, var, xc_done, signal):
                for nt in range(NT):
                    ac.wait_ge(xc_done, nth(a, NT, nt))
                    if nt:
                        ac.wait_ge(signal, nth(a, NT, nt - 1))
                    ac.activation(junk[:, :], xc[:, nt, :], ACT.Square, scale=float(D) ** -0.5,
                                  accum_out=var[:, nt:nt + 1]).then_inc(signal, 1)

            def hT_step(a):
                ac.wait_ge(pe_hT, a + 1)
                ac.wait_ge(pe_u, nth(a, E, -1))
                ac.activation(hT_hi[:, :], used(6), ACT.Copy).then_inc(ac_hT, 1)

            def silu_step(a, e):
                ac.wait_ge(pe_u, nth(a, E, e))
                if e >= 2:
                    ac.wait_ge(dv_actlo, nth(a, E, e - 2))
                else:
                    ac.wait_ge(dv_actlo, nth(a, E, -1))
                ac.activation(act[:, e % 2, :], used(U_BANK[e]), ACT.Silu).then_inc(ac_silu, 1)

            def act_hi_step(a, e):
                ac.wait_ge(dv_act, nth(a, E, e))
                ac.wait_ge(pe_y, nth(a, E, e - 2) if e >= 2 else nth(a, E, -1))
                ac.activation(act_hi[:, e % 2, :], act[:, e % 2, :], ACT.Copy).then_inc(ac_act, 1)

            def var1_step(a):
                ac.wait_ge(ac_ssq, nth(a, NT, -1))
                centred_square(a, var1, dv_xc1, ac_var1)

            def var2_step(a):
                ac.wait_ge(ac_var1, nth(a, NT, NT - 1))
                centred_square(a, var2, dv_xc2, ac_var2)

            def ssq_step(a):
                ac.wait_ge(ac_var2, nth(a, NT, NT - 1))
                for nt in range(NT):
                    ac.wait_ge(dv_xln, nth(a, NT, nt))
                    if nt:
                        ac.wait_ge(ac_ssq, nth(a, NT, nt - 1))
                    ac.activation(junk[:, :], xc[:, nt, :], ACT.Square,
                                  accum_out=ssq[:, nt:nt + 1]).then_inc(ac_ssq, 1)

            def xT_step(a):
                ac.wait_ge(pe_xT, a + 1)
                ac.activation(xT_hi[:, :], used(5), ACT.Copy).then_inc(ac_xT, 1)

            def exp1(b, g):
                c = g // 2
                if is_first(b) and g == 0:
                    ac.wait_ge(pl_w2, 2)
                ac.wait_ge(dv_M1, nth(b, NG, g))
                ac.wait_ge(pe_T2, nth(b, 2 * NCH, 2 * (c - 2) + 1) if c >= 2 else nth(b, 2 * NCH, -1))
                for j in range(2):
                    s = 2 * g + j
                    last = ac.activation(dT[:, c % 2, s % EPC, :], bank[2 + g % 2][:, j * N:(j + 1) * N], ACT.Exp,
                                         bias=nmax_s[:, s:s + 1], accum_out=Z_s[:, s:s + 1])
                last.then_inc(ac_exp1, 1)

            def disp_step(b, c):
                ac.wait_ge(pe_T2, nth(b, 2 * NCH, 2 * c))
                ac.wait_ge(pe_h, nth(b, NCH, c - 2) if c >= 2 else nth(b, NCH, -1))
                ac.activation(disp[:, c % 2, 0, :], used(4), ACT.Copy).then_inc(ac_disp, 1)

            def G_step(b, k):
                ac.wait_ge(pe_G, nth(b, 4, k))
                ac.wait_ge(pe_h, nth(b, NCH, -1))
                if is_first(b):
                    ac.wait_ge(pl_w1, DK)
                ch, nt = k // 2, k % 2
                ac.activation(G[:, nt, ch * CW:(ch + 1) * CW], used(k % 2), ACT.Copy).then_inc(ac_G, 1)

            def exp2(b, c, nt):
                ac.wait_ge(dv_M2, b + 1)
                ac.wait_ge(pe_T1, nth(b, NG, 2 * c + 1))
                part = lg[:, nt, c * CW:(c + 1) * CW]
                ac.activation(part, part, ACT.Exp, bias=nmax_n[:, nt:nt + 1]).then_inc(ac_exp2, 1)

            def gelu_step(b, q):
                ac.wait_ge(pl_hb, nth(b, 2, q))
                ac.activation(hid[:, q, :], hid[:, q, :], ACT.Gelu).then_inc(ac_gelu, 1)

            def h_hi_step(b, q):
                ac.wait_ge(ac_gelu, nth(b, 2, q))
                ac.wait_ge(pe_Q, nth(b, NCH, -1))
                if is_first(b):
                    ac.wait_ge(pl_hzero, 2)
                ac.activation(h_hi[:, 4 * q:4 * q + 4, 0:4:3, :],
                              hid[:, q, :].rearrange("p (j t h) -> p j t h", t=2, h=H), ACT.Copy).then_inc(ac_h, 1)

            def cT_step(b, g):
                ac.wait_ge(pe_T3, nth(b, NG, g))
                ac.wait_ge(pe_Q, nth(b, NCH, g // 2 - 2) if g >= 4 else nth(b, NCH, -1))
                ac.activation(cT_hi[:, g % 4, :, :].rearrange("p j n -> p (j n)"), used(2 + g % 2),
                              ACT.Copy).then_inc(ac_cT, 1)

            def sT_step(b):
                ac.wait_ge(pe_sT, b + 1)
                ac.activation(esumT[:, :], used(4, N), ACT.Copy).then_inc(ac_sT, 1)

            def Q_step(b, c):
                ac.wait_ge(pe_Q, nth(b, NCH, c))
                ac.wait_ge(pe_out, nth(b, NCH, c - 2) if c >= 2 else nth(b, NCH, -1))
                ac.activation(qT_hi[:, c % 2, :], used(c % 2), ACT.Copy).then_inc(ac_Q, 1)

            def sq_step(j):
                c, k = j // DK, j % DK
                ac.wait_ge(ld_mu, 16 * DK)
                if j >= 2:
                    ac.wait_ge(pe_mu_ss, j - 1)
                ac.activation(hid[:, j % 2, :], mu_raw[:, k, c * CW:(c + 1) * CW], ACT.Square).then_inc(ac_sq, 1)

            def mu_hi_step(c, k):
                ac.wait_ge(dv_mun, DK * c + k + 1)
                part = slice(c * CW, (c + 1) * CW)
                ac.activation(mu_hi[:, k, part], mu_raw[:, k, part], ACT.Copy).then_inc(ac_mu, 1)

            def diag_step(c):
                ac.wait_ge(pl_mu_r, 1)
                ac.wait_ge(pe_mu_ss, DK * NCH)
                if c >= 2:
                    ac.wait_ge(pe_mu_bc, c - 1)
                for j in range(EPC):
                    s = c * EPC + j
                    last = ac.activation(hid[:, c % 2, j * P:(j + 1) * P], ident[:, :], ACT.Copy,
                                         scale=mu_ss[:, 2, s:s + 1])
                last.then_inc(ac_diag, 1)

            def ctx_step(e):
                ac.wait_ge(pe_ctxT, e + 1)
                ac.activation(ctxT_hi[:, :, e * F:(e + 1) * F], used(2 + e % 2).rearrange("p (k f) -> p k f", k=DK),
                              ACT.Copy).then_inc(ac_ctx, 1)

            ac.dma_start(gates[:, 0:1], g_xattn.partition_broadcast(P)).then_inc(ld_gates, 16)
            ac.dma_start(gates[:, 1:2], g_ffn.partition_broadcast(P)).then_inc(ld_gates, 16)
            ac.dma_start(gates[:, 2:3], scale.partition_broadcast(P)).then_inc(ld_gates, 16)
            ac.dma_start(ids_raw, ids.rearrange("b n -> (b n)").partition_broadcast(P)).then_inc(ld_ids, 16)
            ac.dma_start(gam[:, :], gamma.partition_broadcast(P)).then_inc(ld_rows, 16)
            ac.dma_start(bet[:, :], beta.partition_broadcast(P)).then_inc(ld_rows, 16)
            ac.dma_start(b1_bc[:, :], b1.rearrange("e h -> (e h)").partition_broadcast(P)).then_inc(ld_rows, 16)
            def w1_hi_step(k):
                ac.wait_ge(ld_w1, 16 * DK)
                ac.activation(w1_hi[:, k, :], w1_raw[:, k, :], ACT.Copy).then_inc(ac_w1, 1)

            def w2_hi_step(j):
                ac.wait_ge(ld_w2, 16)
                part = slice(j * NG // 2, (j + 1) * NG // 2)
                ac.activation(w2_hi[:, part, :], w2_raw[:, part, :], ACT.Copy).then_inc(ac_w2, 1)

            var1_step(0)
            ctx_step(0)
            ac.wait_ge(ld_gates, 48)
            ac.activation(tg[:, :], gates[:, 0:2], ACT.Tanh).then_inc(ac_tg, 1)
            hT_step(0)
            ctx_step(1)
            sq_step(0)
            sq_step(1)
            ctx_step(2)
            ctx_step(3)
            sq_step(2)
            sq_step(3)
            silu_step(0, 0)
            sq_step(4)
            sq_step(5)
            silu_step(0, 1)
            sq_step(6)
            sq_step(7)
            act_hi_step(0, 0)
            act_hi_step(0, 1)
            silu_step(0, 2)
            diag_step(0)
            silu_step(0, 3)
            diag_step(1)
            act_hi_step(0, 2)
            mu_hi_step(0, 0)
            mu_hi_step(0, 1)
            act_hi_step(0, 3)
            diag_step(2)
            mu_hi_step(1, 0)
            mu_hi_step(1, 1)
            diag_step(3)
            w1_hi_step(0)
            var2_step(0)
            w1_hi_step(1)
            mu_hi_step(2, 0)
            mu_hi_step(2, 1)
            ssq_step(0)
            xT_step(0)
            w2_hi_step(0)
            w2_hi_step(1)
            mu_hi_step(3, 0)
            mu_hi_step(3, 1)

            def iteration(b, a):
                if a is not None:
                    var1_step(a)
                for g in range(4):
                    exp1(b, g)
                disp_step(b, 0)
                if a is not None:
                    hT_step(a)
                exp1(b, 4)
                exp1(b, 5)
                disp_step(b, 1)
                G_step(b, 0)
                G_step(b, 1)
                exp1(b, 6)
                exp1(b, 7)
                exp2(b, 0, 0)
                exp2(b, 0, 1)
                disp_step(b, 2)
                exp2(b, 1, 0)
                exp2(b, 1, 1)
                G_step(b, 2)
                G_step(b, 3)
                exp2(b, 2, 0)
                exp2(b, 2, 1)
                disp_step(b, 3)
                exp2(b, 3, 0)
                exp2(b, 3, 1)
                if a is not None:
                    silu_step(a, 0)
                    silu_step(a, 1)
                    act_hi_step(a, 0)
                cT_step(b, 0)
                cT_step(b, 1)
                if a is not None:
                    act_hi_step(a, 1)
                    silu_step(a, 2)
                    silu_step(a, 3)
                cT_step(b, 2)
                cT_step(b, 3)
                if a is not None:
                    act_hi_step(a, 2)
                    act_hi_step(a, 3)
                for q in range(2):
                    gelu_step(b, q)
                    h_hi_step(b, q)
                sT_step(b)
                if a is not None:
                    var2_step(a)
                Q_step(b, 0)
                cT_step(b, 4)
                cT_step(b, 5)
                Q_step(b, 1)
                if a is not None:
                    ssq_step(a)
                cT_step(b, 6)
                cT_step(b, 7)
                Q_step(b, 2)
                Q_step(b, 3)
                if a is not None:
                    xT_step(a)

            iteration(0, 1)
            with ac.Fori(1, B - 1) as b:
                iteration(b, b + 1)
            iteration(B - 1, None)

        @block.vector
        def _(dv):
            def split_lo(out_lo, whole, hi):
                return dv.tensor_tensor(out_lo, whole, as_f32(hi), ALU.subtract)

            def centre1(a):
                dv.wait_ge(pe_xT, nth(a, 1, -1))
                if is_first(a):
                    dv.wait_ge(ld_x0, 16)
                else:
                    dv.wait_ge(ld_x, 16 * (B - 1))
                for nt in range(NT):
                    dv.tensor_scalar(xc[:, nt, :], token_tile(a, nt), 1.0 / D, None, ALU.mult, ALU.add,
                                     accum_out=mean1[:, nt:nt + 1]).then_inc(dv_mean1, 1)
                for nt in range(NT):
                    dv.wait_ge(dv_mean1, nth(a, NT, nt))
                    dv.tensor_scalar(xc[:, nt, :], token_tile(a, nt), mean1[:, nt:nt + 1], None,
                                     ALU.subtract).then_inc(dv_xc1, 1)

            def mask_step(a):
                dv.wait_ge(pl_mask, nth(a, E, -1))
                dv.wait_ge(dv_cls, E - 1)
                for e in range(E):
                    dv.tensor_scalar(mask[:, e, :], cls[:, bass.ds(a * N, N)], e, None,
                                     ALU.is_equal).then_inc(dv_mask, 1)

            def norm1(a):
                dv.wait_ge(ac_var1, nth(a, NT, NT - 1))
                dv.wait_ge(pl_rstd1, nth(a, 2, 1))
                for nt in range(NT):
                    dv.tensor_scalar(xc[:, nt, :], xc[:, nt, :], rstd1[:, 1, nt:nt + 1], None,
                                     ALU.mult).then_inc(dv_hn, 1)

            def hT_step(a):
                dv.wait_ge(ac_hT, a + 1)
                split_lo(hT_lo[:, :], used(6), hT_hi[:, :]).then_inc(dv_hT, 1)

            def act_step(a, e):
                dv.wait_ge(pl_mask, nth(a, E, e))
                dv.tensor_tensor(act[:, e % 2, :], used(U_BANK[e]), act[:, e % 2, :], ALU.mult).then_inc(dv_act, 1)

            def act_lo_step(a, e):
                dv.wait_ge(ac_act, nth(a, E, e))
                split_lo(act_lo[:, e % 2, :], act[:, e % 2, :], act_hi[:, e % 2, :]).then_inc(dv_actlo, 1)

            def x1_step(a):
                dv.wait_ge(ac_tg, 1)
                dv.wait_ge(pe_y, nth(a, E, E - 1))
                for nt in range(NT):
                    dv.scalar_tensor_tensor(out=token_tile(a, nt), in0=used(6 + nt, D), scalar=tg[:, 0:1],
                                            in1=token_tile(a, nt), op0=ALU.mult, op1=ALU.add,
                                            accum_out=sum2[:, 0, nt:nt + 1]).then_inc(dv_x1, 1)
                dv.wait_ge(dv_x1, nth(a, NT, NT - 1))
                dv.tensor_scalar(sum2[:, 1, :], sum2[:, 0, :], -1.0 / D, None, ALU.mult).then_inc(dv_nm2, 1)
                dv.wait_ge(dv_nm2, a + 1)
                for nt in range(NT):
                    dv.tensor_scalar(xc[:, nt, :], token_tile(a, nt), sum2[:, 1, nt:nt + 1], None,
                                     ALU.add).then_inc(dv_xc2, 1)

            def x_ln_step(a):
                dv.wait_ge(ac_var2, nth(a, NT, NT - 1))
                dv.wait_ge(pl_rstd2, nth(a, 3, 2))
                for nt in range(NT):
                    dv.scalar_tensor_tensor(out=xc[:, nt, :], in0=xc[:, nt, :], scalar=rstd2[:, 2, nt:nt + 1],
                                            in1=gam[:, :], op0=ALU.mult, op1=ALU.mult).then_inc(dv_xg, 1)
                for nt in range(NT):
                    dv.wait_ge(dv_xg, nth(a, NT, nt))
                    dv.tensor_tensor(xc[:, nt, :], xc[:, nt, :], bet[:, :], ALU.add).then_inc(dv_xln, 1)

            def ssg_step(a):
                dv.wait_ge(ac_ssq, nth(a, NT, NT - 1))
                dv.wait_ge(pl_rn, nth(a, 2, -1))
                dv.tensor_scalar(ssg[:, :], ssq[:, :], L2_EPS * L2_EPS, None, ALU.max).then_inc(dv_ssg, 1)

            def xT_step(a):
                dv.wait_ge(ac_xT, a + 1)
                split_lo(xT_lo[:, :], used(5), xT_hi[:, :]).then_inc(dv_xT, 1)

            def logits(b, j):
                c, nt = j // 2, j % 2
                dv.wait_ge(pl_rn, nth(b, 2, 1))
                dv.wait_ge(pe_T3, nth(b, NG, -1))
                dv.wait_ge(dv_es, nth(b, NCH, -1))
                if is_first(b) and j == 0:
                    dv.wait_ge(dv_mu, DK * NCH)
                dv.wait_ge(pe_L, nth(b, 2 * NCH, j))
                dv.tensor_scalar(lg[:, nt, c * CW:(c + 1) * CW], used(j % 2), rnorm[:, 1, nt:nt + 1], None,
                                 ALU.mult, ALU.max, accum_out=mx[:, nt, c:c + 1]).then_inc(dv_L, 1)

            def max_s(b, g):
                dv.wait_ge(ac_exp1, nth(b, NG, -1))
                dv.wait_ge(pe_T1, nth(b, NG, g))
                dv.tensor_reduce(nmax_s[:, 2 * g:2 * g + 2], used(2 + g % 2).rearrange("p (j n) -> p j n", j=2),
                                 axis=AX.X, op=ALU.max, negate=True).then_inc(dv_M1, 1)

            def max_n(b):
                dv.wait_ge(dv_L, nth(b, 2 * NCH, 2 * NCH - 1))
                dv.tensor_reduce(nmax_n[:, :], mx[:, :, :], axis=AX.X, op=ALU.max, negate=True).then_inc(dv_M2, 1)

            def disp_step(b, c):
                dv.wait_ge(pe_T2, nth(b, 2 * NCH, 2 * c + 1))
                dv.wait_ge(pe_h, nth(b, NCH, c - 2) if c >= 2 else nth(b, NCH, -1))
                dv.tensor_copy(disp[:, c % 2, 1, :], used(5)).then_inc(dv_disp, 1)

            def rZ_step(b, q):
                dv.wait_ge(ac_exp1, nth(b, NG, 4 * q + 3))
                dv.wait_ge(dv_hs, nth(b, 2, -1))
                half = slice(8 * q, 8 * q + 8)
                dv.reciprocal(rZ_s[:, half], Z_s[:, half]).then_inc(dv_rZ, 1)

            def hidden_scale(b, q):
                dv.wait_ge(dv_rZ, nth(b, 2, q))
                dv.wait_ge(dv_hlo, nth(b, 2, -1))
                dv.wait_ge(pe_h, nth(b, NCH, 2 * q + 1))
                dv.tensor_tensor(hid[:, q, :].rearrange("p (e h) -> p e h", h=H),
                                 used(6 + q).rearrange("p (e h) -> p e h", h=H),
                                 rZ_s[:, 8 * q:8 * q + 8].unsqueeze(2).to_broadcast([P, 8, H]),
                                 ALU.mult).then_inc(dv_hs, 1)

            def hidden_lo(b, q):
                dv.wait_ge(ac_h, nth(b, 2, q))
                split_lo(h_lo[:, 4 * q:4 * q + 4, 0:4:3, :], hid[:, q, :].rearrange("p (j t h) -> p j t h", t=2, h=H),
                         h_hi[:, 4 * q:4 * q + 4, 0:4:3, :]).then_inc(dv_hlo, 1)

            def esum_step(b, c):
                dv.wait_ge(ac_exp2, nth(b, 2 * NCH, 2 * c + 1))
                dv.wait_ge(pe_sT, nth(b, 1, -1))
                dv.wait_ge(dv_Zn, nth(b, 3, -1))
                dv.tensor_reduce(esum_tiles[:, :, c * EPC:(c + 1) * EPC],
                                 lg[:, :, c * CW:(c + 1) * CW].rearrange("p t (e s) -> p t e s", s=S),
                                 axis=AX.X, op=ALU.add).then_inc(dv_es, 1)

            def Zn_step(b):
                dv.wait_ge(dv_es, nth(b, NCH, NCH - 1))
                dv.wait_ge(dv_fin, nth(b, NT, -1))
                dv.tensor_reduce(Z_n[:, 0, :], esum_tiles, axis=AX.X, op=ALU.add).then_inc(dv_Zn, 1)
                dv.wait_ge(dv_Zn, nth(b, 3, 0))
                dv.reciprocal(Z_n[:, 1, :], Z_n[:, 0, :]).then_inc(dv_Zn, 1)
                dv.wait_ge(dv_Zn, nth(b, 3, 1))
                dv.tensor_scalar(Z_n[:, 2, :], Z_n[:, 1, :], tg[:, 1:2], None, ALU.mult).then_inc(dv_Zn, 1)

            def cT_step(b, g):
                dv.wait_ge(ac_cT, nth(b, NG, g))
                split_lo(cT_lo[:, g % 4, :, :].rearrange("p j n -> p (j n)"), used(2 + g % 2),
                         cT_hi[:, g % 4, :, :].rearrange("p j n -> p (j n)")).then_inc(dv_cT, 1)

            def Q_step(b, c):
                dv.wait_ge(ac_Q, nth(b, NCH, c))
                split_lo(qT_lo[:, c % 2, :], used(c % 2), qT_hi[:, c % 2, :]).then_inc(dv_Q, 1)

            def final(b):
                dv.wait_ge(dv_Zn, nth(b, 3, 2))
                dv.wait_ge(pe_out, nth(b, NCH, NCH - 1))
                for nt in range(NT):
                    dv.scalar_tensor_tensor(out=token_tile(b, nt), in0=used(6 + nt, D), scalar=Z_n[:, 2, nt:nt + 1],
                                            in1=token_tile(b, nt), op0=ALU.mult, op1=ALU.add).then_inc(dv_fin, 1)

            def mu_lo_step(c, k):
                dv.wait_ge(ac_mu, DK * c + k + 1)
                part = slice(c * CW, (c + 1) * CW)
                split_lo(mu_lo[:, k, part], mu_raw[:, k, part], mu_hi[:, k, part]).then_inc(dv_mu, 1)

            def ctx_lo_step(e):
                dv.wait_ge(ac_ctx, e + 1)
                part = slice(e * F, (e + 1) * F)
                split_lo(ctxT_lo[:, :, part], used(2 + e % 2).rearrange("p (k f) -> p k f", k=DK),
                         ctxT_hi[:, :, part]).then_inc(dv_ctx, 1)

            def class_step(e):
                if e == 1:
                    dv.tensor_scalar(cls[:, :], ids_f, PER_EXPERT, None, ALU.is_ge).then_inc(dv_cls, 1)
                else:
                    dv.wait_ge(dv_cls, e - 1)
                    dv.scalar_tensor_tensor(out=cls[:, :], in0=ids_f, scalar=e * PER_EXPERT, in1=cls[:, :],
                                            op0=ALU.is_ge, op1=ALU.add).then_inc(dv_cls, 1)

            def mun_step(c, k):
                dv.wait_ge(ld_mu, 16 * DK)
                dv.wait_ge(pe_mu_bc, c + 1)
                part = mu_raw[:, k, c * CW:(c + 1) * CW]
                dv.tensor_tensor(part, used(2 + c % 2), part, ALU.mult).then_inc(dv_mun, 1)

            centre1(0)
            dv.wait_ge(ld_ids, 16)
            dv.tensor_copy(ids_f, ids_raw).then_inc(dv_ids, 1)
            norm1(0)
            dv.wait_ge(dv_ids, 1)
            class_step(1)
            ctx_lo_step(0)
            hT_step(0)
            ctx_lo_step(1)
            class_step(2)
            class_step(3)
            mask_step(0)
            ctx_lo_step(2)
            ctx_lo_step(3)
            act_step(0, 0)
            act_lo_step(0, 0)
            dv.wait_ge(pe_mu_ss, DK * NCH)
            dv.tensor_copy(mu_ss[:, 0, :], bank[7][:, 0:E2]).then_inc(dv_mu_ss, 1)
            dv.wait_ge(dv_mu_ss, 1)
            dv.tensor_tensor(mu_ss[:, 0, :], bank[7][:, E2:2 * E2], mu_ss[:, 0, :], ALU.add).then_inc(dv_mu_ss, 1)
            dv.wait_ge(dv_mu_ss, 2)
            dv.tensor_scalar(mu_ss[:, 1, :], mu_ss[:, 0, :], L2_EPS * L2_EPS, None, ALU.max).then_inc(dv_mu_ss, 1)
            act_step(0, 1)
            act_lo_step(0, 1)
            act_step(0, 2)
            act_lo_step(0, 2)
            mun_step(0, 0)
            mun_step(0, 1)
            act_step(0, 3)
            act_lo_step(0, 3)
            mun_step(1, 0)
            mun_step(1, 1)
            mu_lo_step(0, 0)
            x1_step(0)
            mu_lo_step(0, 1)
            mun_step(2, 0)
            mun_step(2, 1)
            dv.wait_ge(ld_rows, 64)
            x_ln_step(0)
            mun_step(3, 0)
            mun_step(3, 1)
            xT_step(0)
            ssg_step(0)
            for c in range(1, NCH):
                for k in range(DK):
                    mu_lo_step(c, k)

            def iteration(b, a):
                if a is not None:
                    centre1(a)
                logits(b, 0)
                logits(b, 1)
                if a is not None:
                    norm1(a)
                logits(b, 2)
                logits(b, 3)
                max_s(b, 0)
                max_s(b, 1)
                logits(b, 4)
                logits(b, 5)
                max_s(b, 2)
                max_s(b, 3)
                disp_step(b, 0)
                if a is not None:
                    hT_step(a)
                logits(b, 6)
                logits(b, 7)
                max_s(b, 4)
                max_s(b, 5)
                max_n(b)
                disp_step(b, 1)
                rZ_step(b, 0)
                max_s(b, 6)
                max_s(b, 7)
                disp_step(b, 2)
                esum_step(b, 0)
                hidden_scale(b, 0)
                rZ_step(b, 1)
                esum_step(b, 1)
                disp_step(b, 3)
                if a is not None:
                    mask_step(a)
                esum_step(b, 2)
                if a is not None:
                    act_step(a, 0)
                hidden_scale(b, 1)
                if a is not None:
                    act_lo_step(a, 0)
                cT_step(b, 0)
                cT_step(b, 1)
                if a is not None:
                    act_step(a, 1)
                    act_lo_step(a, 1)
                esum_step(b, 3)
                if a is not None:
                    act_step(a, 2)
                cT_step(b, 2)
                cT_step(b, 3)
                if a is not None:
                    act_lo_step(a, 2)
                    act_step(a, 3)
                    act_lo_step(a, 3)
                hidden_lo(b, 0)
                hidden_lo(b, 1)
                if a is not None:
                    x1_step(a)
                Q_step(b, 0)
                cT_step(b, 4)
                cT_step(b, 5)
                if a is not None:
                    x_ln_step(a)
                Q_step(b, 1)
                cT_step(b, 6)
                cT_step(b, 7)
                if a is not None:
                    ssg_step(a)
                Zn_step(b)
                Q_step(b, 2)
                Q_step(b, 3)
                if a is not None:
                    xT_step(a)
                final(b)

            iteration(0, 1)
            with dv.Fori(1, B - 1) as b:
                iteration(b, b + 1)
            iteration(B - 1, None)

        @block.tensor
        def _(pe):
            def mm(out_ap, lhsT, rhs, start, stop):
                return pe.matmul(out_ap, lhsT, rhs, start=start, stop=stop, skip_group_check=True)

            def mm_split(out_ap, lhs, rhs, start, stop):
                mm(out_ap, lhs[0], rhs[0], start, False)
                mm(out_ap, lhs[0], rhs[1], False, False)
                return mm(out_ap, lhs[1], rhs[0], False, stop)

            def hT_transposes(a):
                pe.wait_ge(pl_ident, 1)
                for nt in range(NT):
                    pe.wait_ge(dv_hn, nth(a, NT, nt))
                    for k in range(DK):
                        last = pe.transpose(bank[6][:, k * N + nt * P:k * N + (nt + 1) * P],
                                            xc[:, nt, k * P:(k + 1) * P], ident[:, :])
                last.then_inc(pe_hT, 1)

            def u_step(a, e):
                if e == 0:
                    pe.wait_ge(ac_hT, a + 1)
                    pe.wait_ge(dv_hT, a + 1)
                for f in range(2):
                    for k in range(DK):
                        cols = slice(e * F + f * P, e * F + (f + 1) * P)
                        rows = slice(k * N, (k + 1) * N)
                        last = mm_split(bank[U_BANK[e]][:, f * N:(f + 1) * N],
                                        (ctxT_hi[:, k, cols], ctxT_lo[:, k, cols]),
                                        (hT_hi[:, rows], hT_lo[:, rows]), k == 0, k == DK - 1)
                last.then_inc(pe_u, 1)

            def y_step(a, e):
                pe.wait_ge(ac_act, nth(a, E, e))
                pe.wait_ge(dv_actlo, nth(a, E, e))
                for nt in range(NT):
                    for f in range(2):
                        tok = slice(f * N + nt * P, f * N + (nt + 1) * P)
                        cols = slice(e * F, (e + 1) * F)
                        last = mm_split(used(6 + nt, D), (act_hi[:, e % 2, tok], act_lo[:, e % 2, tok]),
                                        (ctxT_hi[:, f, cols], ctxT_lo[:, f, cols]),
                                        e == 0 and f == 0, e == E - 1 and f == 1)
                last.then_inc(pe_y, 1)

            def xT_transposes(a):
                for nt in range(NT):
                    pe.wait_ge(dv_xln, nth(a, NT, nt))
                    for k in range(DK):
                        last = pe.transpose(bank[5][:, k * N + nt * P:k * N + (nt + 1) * P],
                                            xc[:, nt, k * P:(k + 1) * P], ident[:, :])
                last.then_inc(pe_xT, 1)

            def x_rows(k, nt):
                rows = slice(k * N + nt * P, k * N + (nt + 1) * P)
                return xT_hi[:, rows], xT_lo[:, rows]

            def L_step(b, j):
                c, nt = j // 2, j % 2
                cols = slice(c * CW, (c + 1) * CW)
                if is_first(b):
                    pe.wait_ge(ac_mu, DK * (c + 1))
                    pe.wait_ge(dv_mu, DK * (c + 1))
                if j < 2:
                    pe.wait_ge(ac_xT, b + 1)
                    pe.wait_ge(dv_xT, b + 1)
                    pe.wait_ge(dv_Q, nth(b, NCH, -1))
                else:
                    pe.wait_ge(dv_L, nth(b, 2 * NCH, j - 2))
                for k in range(DK):
                    last = mm_split(used(j % 2), x_rows(k, nt), (mu_hi[:, k, cols], mu_lo[:, k, cols]),
                                    k == 0, k == DK - 1)
                last.then_inc(pe_L, 1)

            def G_step(b, i):
                ch, nt = i // 2, i % 2
                cols = slice(ch * CW, (ch + 1) * CW)
                if i < 2:
                    pe.wait_ge(dv_L, nth(b, 2 * NCH, 6 + i))
                else:
                    pe.wait_ge(ac_G, nth(b, 4, i - 2))
                for k in range(DK):
                    last = mm_split(used(i % 2), x_rows(k, nt), (w1_hi[:, k, cols], w1_lo[:, k, cols]),
                                    k == 0, k == DK - 1)
                last.then_inc(pe_G, 1)

            def T1_step(b, g):
                c = g // 2
                pe.wait_ge(dv_L, nth(b, 2 * NCH, 2 * c + 1))
                if g >= 2:
                    pe.wait_ge(ac_exp1, nth(b, NG, g - 2))
                else:
                    pe.wait_ge(dv_cT, nth(b, NG, -1))
                for j in range(2):
                    for nt in range(NT):
                        s = (2 * g + j) * S
                        last = pe.transpose(bank[2 + g % 2][:, j * N + nt * P:j * N + (nt + 1) * P],
                                            lg[:, nt, s:s + S], ident[:, :])
                last.then_inc(pe_T1, 1)

            def T2_step(b, c):
                pe.wait_ge(ac_exp1, nth(b, NG, 2 * c + 1))
                for nt in range(NT):
                    if nt == 0:
                        pe.wait_ge(ac_sT, nth(b, 1, -1))
                        if c:
                            pe.wait_ge(ac_disp, nth(b, NCH, c - 1))
                    elif c:
                        pe.wait_ge(dv_disp, nth(b, NCH, c - 1))
                    for j in range(EPC):
                        last = pe.transpose(bank[4 + nt][:, j * S:(j + 1) * S],
                                            dT[:, c % 2, j, nt * P:(nt + 1) * P], ident[:, :])
                    last.then_inc(pe_T2, 1)

            def h_step(b, c):
                pe.wait_ge(ac_disp, nth(b, NCH, c))
                pe.wait_ge(dv_disp, nth(b, NCH, c))
                pe.wait_ge(ac_G, nth(b, 4, 2 * (c // 2) + 1))
                pe.wait_ge(dv_fin, nth(b, NT, -1))
                for j in range(EPC):
                    e = c * EPC + j
                    for nt in range(NT):
                        last = mm(bank[6 + c // 2][:, (e % 8) * H:(e % 8 + 1) * H],
                                  disp[:, c % 2, nt, j * S:(j + 1) * S], G[:, nt, e * H:(e + 1) * H],
                                  nt == 0, nt == NT - 1)
                last.then_inc(pe_h, 1)

            def T3_step(b, g):
                pe.wait_ge(ac_exp2, nth(b, 2 * NCH, 2 * (g // 2) + 1))
                if g >= 2:
                    pe.wait_ge(dv_cT, nth(b, NG, g - 2))
                else:
                    pe.wait_ge(ac_exp1, nth(b, NG, 6 + g))
                for j in range(2):
                    for nt in range(NT):
                        s = (2 * g + j) * S
                        last = pe.transpose(bank[2 + g % 2][:, j * N + nt * P:j * N + (nt + 1) * P],
                                            lg[:, nt, s:s + S], ident[:, :])
                last.then_inc(pe_T3, 1)

            def Q_step(b, c):
                pe.wait_ge(ac_h, nth(b, 2, c // 2))
                pe.wait_ge(dv_hlo, nth(b, 2, c // 2))
                pe.wait_ge(dv_cT, nth(b, NG, 2 * c + 1))
                if c >= 2:
                    pe.wait_ge(dv_Q, nth(b, NCH, c - 2))
                for i in range(2):
                    p = 2 * c + i
                    for t in range(2):
                        lhs = [w[:, p, 2 * t:2 * t + 2, :].rearrange("p a h -> p (a h)") for w in (h_hi, h_lo)]
                        last = mm_split(bank[c % 2][:, i * N:(i + 1) * N], lhs,
                                        (cT_hi[:, p % 4, t, :], cT_lo[:, p % 4, t, :]), t == 0, t == 1)
                last.then_inc(pe_Q, 1)

            def sT_transposes(b):
                pe.wait_ge(dv_es, nth(b, NCH, NCH - 1))
                pe.wait_ge(ac_disp, nth(b, NCH, NCH - 1))
                for nt in range(NT):
                    last = pe.transpose(bank[4][:, nt * P:(nt + 1) * P], esum[:, nt * E2:nt * E2 + P], ident[:, :])
                last.then_inc(pe_sT, 1)

            def out_step(b, c):
                if c == 0:
                    pe.wait_ge(ac_sT, b + 1)
                    for nt in range(NT):
                        mm(used(6 + nt, D), esumT[:, nt * P:(nt + 1) * P], b2_pad[:, :], True, False)
                pe.wait_ge(ac_Q, nth(b, NCH, c))
                pe.wait_ge(dv_Q, nth(b, NCH, c))
                for i in range(2):
                    p = 2 * c + i
                    for nt in range(NT):
                        rows = slice(i * N + nt * P, i * N + (nt + 1) * P)
                        last = mm_split(used(6 + nt, D), (qT_hi[:, c % 2, rows], qT_lo[:, c % 2, rows]),
                                        (w2_hi[:, p, :], w2_lo[:, p, :]), False, p == NG - 1)
                last.then_inc(pe_out, 1)

            def ctx_transposes(e):
                pe.wait_ge(pl_ident, 1)
                pe.wait_ge(ld_ctx[e], 16)
                if e >= 2:
                    pe.wait_ge(dv_ctx, e - 1)
                for f in range(2):
                    for k in range(DK):
                        last = pe.transpose(bank[2 + e % 2][:, k * F + f * P:k * F + (f + 1) * P],
                                            ctx_raw[:, e * 2 + f, k * P:(k + 1) * P], ident[:, :])
                last.then_inc(pe_ctxT, 1)

            def mu_squares(c):
                pe.wait_ge(pl_const, 7)
                for k in range(DK):
                    pe.wait_ge(ac_sq, DK * c + k + 1)
                    for j in range(EPC):
                        s = k * E2 + c * EPC + j
                        last = mm(bank[7][:, s:s + 1], hid[:, k, j * P:(j + 1) * P], ones[:, 0:1], True, True)
                    last.then_inc(pe_mu_ss, 1)

            def mu_spread(c):
                pe.wait_ge(ac_diag, c + 1)
                if c >= 2:
                    pe.wait_ge(dv_mun, DK * (c - 1))
                mm(used(2 + c % 2), ones[:, :], hid[:, c % 2, :], True, True).then_inc(pe_mu_bc, 1)

            def ctx_ready(e):
                pe.wait_ge(ac_ctx, e + 1)
                pe.wait_ge(dv_ctx, e + 1)

            ctx_transposes(0)
            hT_transposes(0)
            ctx_transposes(1)
            ctx_ready(0)
            u_step(0, 0)
            ctx_transposes(2)
            ctx_transposes(3)
            mu_squares(0)
            ctx_ready(1)
            u_step(0, 1)
            mu_squares(1)
            ctx_ready(2)
            u_step(0, 2)
            mu_squares(2)
            ctx_ready(3)
            u_step(0, 3)
            mu_squares(3)
            pe.wait_ge(dv_mu_ss, 2)
            y_step(0, 0)
            y_step(0, 1)
            mu_spread(0)
            y_step(0, 2)
            mu_spread(1)
            y_step(0, 3)
            mu_spread(2)
            mu_spread(3)
            xT_transposes(0)

            def iteration(b, a):
                for j in range(4):
                    L_step(b, j)
                T1_step(b, 0)
                T1_step(b, 1)
                L_step(b, 4)
                L_step(b, 5)
                T1_step(b, 2)
                T1_step(b, 3)
                T2_step(b, 0)
                if a is not None:
                    hT_transposes(a)
                L_step(b, 6)
                L_step(b, 7)
                T1_step(b, 4)
                T1_step(b, 5)
                T2_step(b, 1)
                if is_first(b):
                    pe.wait_ge(ac_w1, DK)
                    pe.wait_ge(pl_w1, DK)
                G_step(b, 0)
                G_step(b, 1)
                T1_step(b, 6)
                T1_step(b, 7)
                if a is not None:
                    pe.wait_ge(dv_hT, a + 1)
                h_step(b, 0)
                T2_step(b, 2)
                G_step(b, 2)
                G_step(b, 3)
                h_step(b, 1)
                T2_step(b, 3)
                pe.wait_ge(ac_G, nth(b, 4, 3))
                if a is not None:
                    u_step(a, 0)
                    u_step(a, 1)
                h_step(b, 2)
                h_step(b, 3)
                pe.wait_ge(dv_disp, nth(b, NCH, NCH - 1))
                if a is not None:
                    u_step(a, 2)
                    u_step(a, 3)
                T3_step(b, 0)
                T3_step(b, 1)
                pe.wait_ge(dv_hs, nth(b, 2, 1))
                if a is not None:
                    y_step(a, 0)
                    y_step(a, 1)
                T3_step(b, 2)
                T3_step(b, 3)
                if a is not None:
                    y_step(a, 2)
                    y_step(a, 3)
                sT_transposes(b)
                T3_step(b, 4)
                T3_step(b, 5)
                Q_step(b, 0)
                Q_step(b, 1)
                T3_step(b, 6)
                T3_step(b, 7)
                if a is not None:
                    pe.wait_ge(dv_x1, nth(a, NT, NT - 1))
                if is_first(b):
                    pe.wait_ge(ac_w2, 2)
                    pe.wait_ge(pl_w2, 2)
                    pe.wait_ge(ld_rows, 64)
                out_step(b, 0)
                Q_step(b, 2)
                out_step(b, 1)
                Q_step(b, 3)
                if a is not None:
                    xT_transposes(a)
                out_step(b, 2)
                out_step(b, 3)

            iteration(0, 1)
            with pe.Fori(1, B - 1) as b:
                iteration(b, b + 1)
            iteration(B - 1, None)


_INS = ["x", "itok_BxS_13_99985", "ctx_2048", "g_xattn", "g_ffn", "L0_ffn_gamma", "L0_ffn_beta", "L0_ffn_mu",
        "L0_ffn_scale", "L0_ffn_W1", "L0_ffn_b1", "L0_ffn_W2", "L0_ffn_b2"]


def kernel(**inputs):
    import numpy as np
    import concourse.bacc as bacc
    from concourse.bass_utils import run_bass_kernel_spmd

    nc = bacc.Bacc("TRN2", target_bir_lowering=False, num_devices=1)
    arrays, args = {}, []
    for name in _INS:
        a = np.ascontiguousarray(inputs[name])
        arrays[f"in_{name}"] = a
        args.append(nc.dram_tensor(f"in_{name}", a.shape, mybir.dt.from_np(a.dtype), kind="ExternalInput").ap())
    out = nc.dram_tensor("out_x", inputs["x"].shape, F32, kind="ExternalOutput").ap()
    flamingo_kernel(nc, *args, out)
    r = run_bass_kernel_spmd(nc, [arrays], core_ids=[0])
    return r.results[0]["out_x"]
```

```python
from contextlib import ExitStack

import concourse.bass as bass
from concourse import mybir

F32 = mybir.dt.float32
F32R = mybir.dt.float32r
I32 = mybir.dt.int32
U8 = mybir.dt.uint8
ALU = mybir.AluOpType
ACT = mybir.ActivationFunctionType
AX = mybir.AxisListType

P = 128
VOCAB = 12500
LN_EPS = 1e-5
L2_EPS = 1e-12


def is_first(b):
    return isinstance(b, int) and b == 0


def nth(b, per_batch, j):
    return b * per_batch + (j + 1)


def flamingo_kernel(nc, x, ids, ctx, g_xattn, g_ffn, gamma, beta, mu, scale, W1, b1, W2, b2, out):
    B, N, D = x.shape
    E, F, _ = ctx.shape
    _, E2, S = mu.shape
    H = W1.shape[2]
    NT = N // P
    DK = D // P
    ES = E2 * S
    EH = E2 * H
    CW = 512
    NCH = ES // CW
    EPC = CW // S
    GR = 32
    NG = E2 // 2
    PER_EXPERT = VOCAB // E
    assert (NT, DK, S, 2 * H, F, E, EPC) == (2, 2, P, P, D, 4, 4)

    es = ExitStack()
    with es:
        def sb(name, shape, dt=F32):
            return es.enter_context(nc.sbuf_tensor(name, shape, dt))

        def sem(name):
            return es.enter_context(nc.semaphore(name))

        x_all = sb("x_all", [P, B * NT, D])
        xc = sb("xc", [P, NT, D])
        hT_hi = sb("hT_hi", [P, DK * N], F32R)
        hT_lo = sb("hT_lo", [P, DK * N], F32R)
        ctxT_hi = sb("ctxT_hi", [P, DK, E * F], F32R)
        ctxT_lo = sb("ctxT_lo", [P, DK, E * F], F32R)
        act = sb("act", [P, 2, 2 * N])
        act_hi = sb("act_hi", [P, 2, 2 * N], F32R)
        act_lo = sb("act_lo", [P, 2, 2 * N], F32R)
        xT_hi = sb("xT_hi", [P, DK * N], F32R)
        xT_lo = sb("xT_lo", [P, DK * N], F32R)
        mu_hi = sb("mu_hi", [P, DK, ES], F32R)
        mu_lo = sb("mu_lo", [P, DK, ES], F32R)
        w1_hi = sb("w1_hi", [P, DK, EH], F32R)
        w1_lo = sb("w1_lo", [P, DK, EH], F32R)
        w2_hi = sb("w2_hi", [P, NG, D], F32R)
        w2_lo = sb("w2_lo", [P, NG, D], F32R)
        b1_bc = sb("b1_bc", [P, EH])
        b2_raw = sb("b2_raw", [P, D])
        b2_parts = sb("b2_parts", [P, D], F32R)
        gam = sb("gam", [P, D])
        bet = sb("bet", [P, D])
        ident = sb("ident", [P, P])
        G = sb("G", [P, NT, EH])
        lg = sb("lg", [P, NT, ES])
        dT = sb("dT", [P, 2, EPC, N])
        disp = sb("disp", [P, 2, NT, CW])
        cT_hi = sb("cT_hi", [P, 4, 2, N], F32R)
        cT_lo = sb("cT_lo", [P, 4, 2, N], F32R)
        hid = sb("hid", [P, 2, CW])
        h_hi = sb("h_hi", [P, NG, 4, H], F32R)
        h_lo = sb("h_lo", [P, NG, 4, H], F32R)
        qT_hi = sb("qT_hi", [P, 2, 2 * N], F32R)
        qT_lo = sb("qT_lo", [P, 2, 2 * N], F32R)
        esum = sb("esum", [P, NT, E2])
        esum_parts = sb("esum_parts", [P, NT, P], F32R)
        esumT = sb("esumT", [P, N], F32R)
        ones = b1_bc[:, 0:P]
        junk = sb("junk", [P, D], U8)
        columns = sb("columns", [P, 180])
        taken = [0]

        def cols(*shape):
            n = shape[0] * (shape[1] if len(shape) > 1 else 1)
            part = columns[:, taken[0]:taken[0] + n]
            taken[0] += n
            return part if len(shape) == 1 else part.rearrange("p (a b) -> p a b", b=shape[1])

        gates = cols(3)
        tg = cols(2)
        scale2 = cols(NT)
        c_eps, c_eps2, c_mhalf = cols(NT), cols(NT), cols(E2)
        ids_raw, ids_f, cls = cols(B * NT), cols(B * NT), cols(B * NT)
        pick = cols(E, NT)
        warm = cols(2)
        mean1, var1, rstd1 = cols(NT), cols(NT), cols(2, NT)
        sum2, var2, rstd2 = cols(2, NT), cols(NT), cols(2, NT)
        ssq, ssg, rnorm = cols(NT), cols(NT), cols(2, NT)
        mx, nmax_n = cols(NT, NCH), cols(NT)
        per_slot = cols(3, E2)
        nmax_s, Z_s, rZ_s = (per_slot[:, i, :] for i in range(3))
        Z_n = cols(3, NT)

        def as_f32(ap):
            return ap.bitcast(F32)

        ctx_raw = dT[:, :, :, :].rearrange("p a b c -> p (a b c)").rearrange("p (k d) -> p k d", d=D)
        w1_raw = G
        mu_sq = dT[:, :, :, :].rearrange("p a b c -> p (a b c)").rearrange("p (k c) -> p k c", k=DK)
        mu_raw = lg
        mu_ss = per_slot
        disp_flat = disp[:, :, :, :].rearrange("p a b c -> p (a b c)")
        w2_raw = disp_flat.rearrange("p (k d) -> p k d", d=D)

        bank = [es.enter_context(nc.psum_tensor(f"bank{i}", [P, CW], F32)) for i in range(8)]

        U_BANK = (0, 1, 4, 5)
        Y_BANK = (6, 7, 6, 7)
        T3_BANK = (2, 3, 4, 5)
        HT_BANK, XT_BANK, ST_BANK = 6, 3, 2
        MU_BC_BANK = (2, 4, 5, 7)
        MU_SS_BANK = (3, 0, 1, 6)

        ld_x0, ld_x, ld_ids, ld_w1, ld_w2, ld_gates, ld_rows, ld_b1, ld_b2 = map(
            sem, ("ld_x0", "ld_x", "ld_ids", "ld_w1", "ld_w2", "ld_gates", "ld_rows", "ld_b1", "ld_b2"))
        ld_mu = [sem(f"ld_mu{c}") for c in range(NCH)]
        ld_ctx = [sem(f"ld_ctx{e}") for e in range(E)]
        stored = sem("stored")
        (pl_zero, pl_ident, pl_const, pl_scale, pl_w1, pl_w2, pl_mu_r, pl_diag, pl_mu, pl_rstd1, pl_hb, pl_hzero,
         pl_rstd2, pl_rn) = map(sem, (
            "pl_zero", "pl_ident", "pl_const", "pl_scale", "pl_w1", "pl_w2", "pl_mu_r", "pl_diag", "pl_mu",
            "pl_rstd1", "pl_hb", "pl_hzero", "pl_rstd2", "pl_rn"))
        (pe_ctxT, pe_mu_ss, pe_mu_bc, pe_hT, pe_u, pe_y, pe_xT, pe_L, pe_T1, pe_T2, pe_G, pe_h, pe_T3, pe_Q, pe_sT,
         pe_out) = map(sem, (
            "pe_ctxT", "pe_mu_ss", "pe_mu_bc", "pe_hT", "pe_u", "pe_y", "pe_xT", "pe_L", "pe_T1", "pe_T2", "pe_G",
            "pe_h", "pe_T3", "pe_Q", "pe_sT", "pe_out"))
        (ac_warm, ac_b2, ac_w1, ac_w2, ac_ctx, ac_tg, ac_sq, ac_mu, ac_var1, ac_hT, ac_silu, ac_act, ac_var2, ac_ssq,
         ac_xT, ac_exp1, ac_disp, ac_G, ac_exp2, ac_gelu, ac_h, ac_cT, ac_Q, ac_sT) = map(sem, (
            "ac_warm", "ac_b2", "ac_w1", "ac_w2", "ac_ctx", "ac_tg", "ac_sq", "ac_mu", "ac_var1", "ac_hT",
            "ac_silu", "ac_act", "ac_var2", "ac_ssq", "ac_xT", "ac_exp1", "ac_disp", "ac_G", "ac_exp2", "ac_gelu",
            "ac_h", "ac_cT", "ac_Q", "ac_sT"))
        (dv_ids, dv_cls, dv_pick, dv_ctx, dv_mu_ss, dv_mun, dv_mu, dv_mean1, dv_xc1, dv_hn, dv_hT, dv_act, dv_actlo,
         dv_x1, dv_nm2, dv_xc2, dv_xg, dv_xln, dv_ssg, dv_xT, dv_L, dv_M1, dv_M2, dv_disp, dv_rZ, dv_hs, dv_es,
         dv_Zn, dv_hlo, dv_ep, dv_b2, dv_cT, dv_Q, dv_fin) = map(sem, (
            "dv_ids", "dv_cls", "dv_pick", "dv_ctx", "dv_mu_ss", "dv_mun", "dv_mu", "dv_mean1", "dv_xc1", "dv_hn",
            "dv_hT", "dv_act", "dv_actlo", "dv_x1", "dv_nm2", "dv_xc2", "dv_xg", "dv_xln", "dv_ssg", "dv_xT",
            "dv_L", "dv_M1", "dv_M2", "dv_disp", "dv_rZ", "dv_hs", "dv_es", "dv_Zn", "dv_hlo", "dv_ep", "dv_b2",
            "dv_cT", "dv_Q", "dv_fin"))

        def mu_lo_done(c):
            return (dv_mu, DK * (1 + c // 3)) if c in (0, 3) else (pl_mu, DK * c)

        def token_tile(b, nt):
            return x_all[:, bass.ds(b * NT + nt, 1), :].rearrange("p a d -> p (a d)")

        def used(ring_bank, n=CW):
            return bank[ring_bank][:, 0:n]

        block = es.enter_context(nc.Block())

        @block.sync
        def _(sp):
            def load_x(b, done):
                sp.dma_start(x_all[:, b * NT:(b + 1) * NT, :],
                             x[b].rearrange("(t p) d -> p t d", p=P)).then_inc(done, 16)

            load_x(0, ld_x0)
            for e in range(E):
                sp.dma_start(ctx_raw[:, 2 * e:2 * e + 2, :],
                             ctx[e].rearrange("(f p) d -> p f d", p=P)).then_inc(ld_ctx[e], 16)
            for c in range(NCH):
                sp.dma_start(mu_raw[:, :, c * CW:(c + 1) * CW],
                             mu[:, c * EPC:(c + 1) * EPC].rearrange("(k p) e s -> p k (e s)", p=P)
                             ).then_inc(ld_mu[c], 16)
                if c == 0:
                    sp.dma_start(ids_raw.bitcast(I32), ids).then_inc(ld_ids, 16)
            sp.dma_start(gam[:, :], gamma.partition_broadcast(P)).then_inc(ld_rows, 16)
            sp.dma_start(bet[:, :], beta.partition_broadcast(P)).then_inc(ld_rows, 16)
            for k in range(DK):
                sp.dma_start(w1_raw[:, k, :].rearrange("p (e h) -> p e h", h=H),
                             W1[:, k * P:(k + 1) * P, :].rearrange("e p h -> p e h")).then_inc(ld_w1, 16)
            for b in range(1, B):
                load_x(b, ld_x)
            sp.dma_start(w2_raw, W2.rearrange("(j two) h d -> (two h) j d", two=2)).then_inc(ld_w2, 16)
            sp.wait_ge(pl_const, 6)
            for i in range(3):
                sp.dma_start(b2_raw[i * GR:i * GR + E2, :], b2).then_inc(ld_b2, 16)
            sp.wait_ge(pe_mu_bc, NCH)
            sp.dma_start(b1_bc[:, :], b1.rearrange("e h -> (e h)").partition_broadcast(P)).then_inc(ld_b1, 16)
            with sp.Fori(0, B) as b:
                for nt in range(NT):
                    sp.wait_ge(dv_fin, nth(b, NT, nt))
                    sp.dma_start(out[bass.ds(b, 1), nt * P:(nt + 1) * P].rearrange("a p d -> p a d"),
                                 x_all[:, bass.ds(b * NT + nt, 1), :]).then_inc(stored, 16)
            sp.wait_ge(stored, 16 * B * NT)

        @block.gpsimd
        def _(pool):
            pool.memset(ident[:, :], 0.0).then_inc(pl_zero, 1)
            pool.wait_ge(pl_zero, 1)
            pool.affine_select(out=ident[:, :], in_=ident[:, :], compare_op=ALU.not_equal, fill=1.0, base=0,
                               pattern=[[-1, P]], channel_multiplier=1).then_inc(pl_ident, 1)
            for tile, value in ((c_eps, LN_EPS), (c_eps2, LN_EPS * LN_EPS),
                                (c_mhalf, -0.5), (ones, 1.0), (as_f32(esum_parts[:, :, :]), 0.0), (b2_raw[:, :], 0.0)):
                pool.memset(tile, value).then_inc(pl_const, 1)
            pool.wait_ge(pl_const, 6)

            def rstd1_step(a):
                pool.wait_ge(ac_var1, nth(a, NT, NT - 1))
                pool.tensor_tensor(rstd1[:, 0, :], var1[:, :], c_eps[:, :], ALU.add).then_inc(pl_rstd1, 1)
                pool.wait_ge(pl_rstd1, nth(a, 2, 0))
                pool.tensor_tensor(rstd1[:, 1, :], rstd1[:, 0, :], c_mhalf[:, 0:NT], ALU.pow).then_inc(pl_rstd1, 1)

            def rstd2_step(a):
                pool.wait_ge(ac_var2, nth(a, NT, NT - 1))
                pool.tensor_tensor(rstd2[:, 0, :], var2[:, :], c_eps2[:, :], ALU.add).then_inc(pl_rstd2, 1)
                pool.wait_ge(pl_rstd2, nth(a, 2, 0))
                pool.tensor_tensor(rstd2[:, 1, :], rstd2[:, 0, :], c_mhalf[:, 0:NT], ALU.pow).then_inc(pl_rstd2, 1)

            def rnorm_step(a):
                pool.wait_ge(dv_ssg, a + 1)
                pool.tensor_tensor(rnorm[:, 0, :], ssg[:, :], c_mhalf[:, 0:NT], ALU.pow).then_inc(pl_rn, 1)
                pool.wait_ge(pl_rn, nth(a, 2, 0))
                if is_first(a):
                    pool.wait_ge(pl_scale, NT)
                pool.tensor_tensor(rnorm[:, 1, :], rnorm[:, 0, :], scale2[:, :], ALU.mult).then_inc(pl_rn, 1)

            def hidden_bias(b, q):
                pool.wait_ge(dv_hs, nth(b, 2, q))
                part = hid[:, q, :]
                pool.tensor_tensor(part, part, b1_bc[:, q * CW:(q + 1) * CW], ALU.add).then_inc(pl_hb, 1)

            def mu_r_step(c):
                part = slice(c * EPC, (c + 1) * EPC)
                pool.wait_ge(dv_mu_ss, c + 1)
                pool.tensor_tensor(mu_ss[:, 1, part], mu_ss[:, 0, part], c_mhalf[:, 0:EPC],
                                   ALU.pow).then_inc(pl_mu_r, 1)
                pool.wait_ge(pl_mu_r, c + 1)
                if c >= 2:
                    pool.wait_ge(pe_mu_bc, c - 1)
                pool.tensor_tensor(hid[:, c % 2, :].rearrange("p (j s) -> p j s", s=P),
                                   ident[:, :].unsqueeze(1).to_broadcast([P, EPC, P]),
                                   mu_ss[:, 1, part].unsqueeze(2).to_broadcast([P, EPC, P]),
                                   ALU.mult).then_inc(pl_diag, 1)

            def mu_lo_step(c):
                for k in range(DK):
                    pool.wait_ge(ac_mu, DK * c + k + 1)
                    part = slice(c * CW, (c + 1) * CW)
                    pool.tensor_tensor(mu_lo[:, k, part], mu_raw[:, k, part], as_f32(mu_hi[:, k, part]),
                                       ALU.subtract).then_inc(pl_mu, 1)

            def w1_lo_step(k):
                pool.wait_ge(ac_w1, k + 1)
                pool.tensor_tensor(w1_lo[:, k, :], w1_raw[:, k, :], as_f32(w1_hi[:, k, :]),
                                   ALU.subtract).then_inc(pl_w1, 1)

            def w2_lo_step(j):
                pool.wait_ge(ac_w2, j // 2 + 1)
                part = slice(j * NG // 4, (j + 1) * NG // 4)
                pool.tensor_tensor(w2_lo[:, part, :], w2_raw[:, part, :], as_f32(w2_hi[:, part, :]),
                                   ALU.subtract).then_inc(pl_w2, 1)

            rstd1_step(0)
            pool.wait_ge(ld_gates, 48)
            for nt in range(NT):
                pool.tensor_copy(scale2[:, nt:nt + 1], gates[:, 2:3]).then_inc(pl_scale, 1)
            mu_r_step(0)
            rstd2_step(0)
            mu_r_step(1)
            mu_r_step(2)
            rnorm_step(0)

            def iteration(b, a):
                if is_first(b):
                    mu_lo_step(1)
                    w2_lo_step(0)
                    mu_lo_step(2)
                    mu_r_step(3)
                if a is not None:
                    rstd1_step(a)
                if is_first(b):
                    for j in range(1, 4):
                        w2_lo_step(j)
                    for k in range(DK):
                        w1_lo_step(k)
                    for tile in (h_hi, h_lo):
                        pool.memset(as_f32(tile[:, :, :, :]), 0.0).then_inc(pl_hzero, 1)
                    pool.wait_ge(ld_b1, 16)
                hidden_bias(b, 0)
                hidden_bias(b, 1)
                if a is not None:
                    rstd2_step(a)
                    rnorm_step(a)

            iteration(0, 1)
            with pool.Fori(1, B - 1) as b:
                iteration(b, b + 1)
            iteration(B - 1, None)

        @block.scalar
        def _(ac):
            def centred_square(a, var, xc_done, signal, factor=1.0):
                for nt in range(NT):
                    ac.wait_ge(xc_done, nth(a, NT, nt))
                    if nt:
                        ac.wait_ge(signal, nth(a, NT, nt - 1))
                    ac.activation(junk[:, :], xc[:, nt, :], ACT.Square, scale=(factor / D) ** 0.5,
                                  accum_out=var[:, nt:nt + 1]).then_inc(signal, 1)

            def hT_step(a):
                ac.wait_ge(pe_hT, a + 1)
                ac.wait_ge(pe_u, nth(a, E, -1))
                ac.activation(hT_hi[:, :], used(HT_BANK), ACT.Copy).then_inc(ac_hT, 1)

            def silu_step(a, e):
                ac.wait_ge(pe_u, nth(a, E, e))
                if e >= 2:
                    ac.wait_ge(dv_actlo, nth(a, E, e - 2))
                else:
                    ac.wait_ge(dv_actlo, nth(a, E, -1))
                ac.activation(act[:, e % 2, :], used(U_BANK[e]), ACT.Silu).then_inc(ac_silu, 1)

            def act_hi_step(a, e):
                ac.wait_ge(dv_act, nth(a, E, e))
                ac.wait_ge(pe_y, nth(a, E, e - 2) if e >= 2 else nth(a, E, -1))
                ac.activation(act_hi[:, e % 2, :], act[:, e % 2, :], ACT.Copy).then_inc(ac_act, 1)

            def var1_step(a):
                ac.wait_ge(ac_ssq, nth(a, NT, -1))
                centred_square(a, var1, dv_xc1, ac_var1)

            def var2_step(a):
                ac.wait_ge(ac_var1, nth(a, NT, NT - 1))
                centred_square(a, var2, dv_xc2, ac_var2, 1.0 + LN_EPS)

            def ssq_step(a):
                ac.wait_ge(ac_var2, nth(a, NT, NT - 1))
                for nt in range(NT):
                    ac.wait_ge(dv_xln, nth(a, NT, nt))
                    if nt:
                        ac.wait_ge(ac_ssq, nth(a, NT, nt - 1))
                    ac.activation(junk[:, :], xc[:, nt, :], ACT.Square,
                                  accum_out=ssq[:, nt:nt + 1]).then_inc(ac_ssq, 1)

            def xT_step(a):
                ac.wait_ge(pe_xT, a + 1)
                ac.activation(xT_hi[:, :], used(XT_BANK), ACT.Copy).then_inc(ac_xT, 1)

            def exp1(b, g):
                c = g // 2
                ac.wait_ge(dv_M1, nth(b, NG, g))
                ac.wait_ge(pe_T2, nth(b, 2 * NCH, 2 * (c - 2) + 1) if c >= 2 else nth(b, 2 * NCH, -1))
                for j in range(2):
                    s = 2 * g + j
                    last = ac.activation(dT[:, c % 2, s % EPC, :], bank[2 + g % 2][:, j * N:(j + 1) * N], ACT.Exp,
                                         bias=nmax_s[:, s:s + 1], accum_out=Z_s[:, s:s + 1])
                last.then_inc(ac_exp1, 1)

            def disp_step(b, c):
                ac.wait_ge(pe_T2, nth(b, 2 * NCH, 2 * c))
                ac.wait_ge(pe_h, nth(b, NCH, c - 2) if c >= 2 else nth(b, NCH, -1))
                if is_first(b):
                    ac.wait_ge(pl_w2, 4)
                ac.activation(disp[:, c % 2, 0, :], used(4), ACT.Copy).then_inc(ac_disp, 1)

            def G_step(b, k):
                ac.wait_ge(pe_G, nth(b, 4, k))
                ac.wait_ge(pe_h, nth(b, NCH, -1))
                ch, nt = k // 2, k % 2
                if is_first(b):
                    ac.wait_ge(pl_w1, DK)
                ac.activation(G[:, nt, ch * CW:(ch + 1) * CW], used(k % 2), ACT.Copy).then_inc(ac_G, 1)

            def exp2(b, c, nt):
                ac.wait_ge(dv_M2, b + 1)
                ac.wait_ge(pe_T1, nth(b, NG, 2 * c + 1))
                part = lg[:, nt, c * CW:(c + 1) * CW]
                ac.activation(part, part, ACT.Exp, bias=nmax_n[:, nt:nt + 1]).then_inc(ac_exp2, 1)

            def gelu_step(b, q):
                ac.wait_ge(pl_hb, nth(b, 2, q))
                ac.activation(hid[:, q, :], hid[:, q, :], ACT.Gelu).then_inc(ac_gelu, 1)

            def h_hi_step(b, q):
                ac.wait_ge(ac_gelu, nth(b, 2, q))
                ac.wait_ge(pe_Q, nth(b, NCH, -1))
                if is_first(b):
                    ac.wait_ge(pl_hzero, 2)
                ac.activation(h_hi[:, 4 * q:4 * q + 4, 0:4:3, :],
                              hid[:, q, :].rearrange("p (j t h) -> p j t h", t=2, h=H), ACT.Copy).then_inc(ac_h, 1)

            def cT_step(b, g):
                ac.wait_ge(pe_T3, nth(b, NG, g))
                ac.wait_ge(pe_Q, nth(b, NCH, g // 2 - 2) if g >= 4 else nth(b, NCH, -1))
                ac.activation(cT_hi[:, g % 4, :, :].rearrange("p j n -> p (j n)"), used(T3_BANK[g % 4]),
                              ACT.Copy).then_inc(ac_cT, 1)

            def sT_step(b):
                ac.wait_ge(pe_sT, b + 1)
                ac.activation(esumT[:, :], used(ST_BANK, N), ACT.Copy).then_inc(ac_sT, 1)

            def Q_step(b, c):
                ac.wait_ge(pe_Q, nth(b, NCH, c))
                ac.wait_ge(pe_out, nth(b, NCH * NT, NT * (c - 2) + NT - 1) if c >= 2 else nth(b, NCH * NT, -1))
                ac.activation(qT_hi[:, c % 2, :], used(c % 2), ACT.Copy).then_inc(ac_Q, 1)

            def sq_step(j):
                c, k = j // DK, j % DK
                ac.wait_ge(ld_mu[c], 16)
                if c >= 2:
                    ac.wait_ge(pe_mu_ss, c - 1)
                else:
                    ac.wait_ge(pe_ctxT, E)
                ac.activation(mu_sq[:, k, (c % 2) * CW:(c % 2 + 1) * CW], mu_raw[:, k, c * CW:(c + 1) * CW],
                              ACT.Square).then_inc(ac_sq, 1)

            def mu_hi_step(c, k):
                ac.wait_ge(dv_mun, DK * c + k + 1)
                part = slice(c * CW, (c + 1) * CW)
                ac.activation(mu_hi[:, k, part], mu_raw[:, k, part], ACT.Copy).then_inc(ac_mu, 1)

            def ctx_step(e):
                ac.wait_ge(pe_ctxT, e + 1)
                ac.activation(ctxT_hi[:, :, e * F:(e + 1) * F], used(2 + e % 2).rearrange("p (k f) -> p k f", k=DK),
                              ACT.Copy).then_inc(ac_ctx, 1)

            def w1_hi_step(k):
                ac.wait_ge(ld_w1, 16 * DK)
                ac.activation(w1_hi[:, k, :], w1_raw[:, k, :], ACT.Copy).then_inc(ac_w1, 1)

            def w2_hi_step(j):
                ac.wait_ge(ld_w2, 16)
                part = slice(j * NG // 2, (j + 1) * NG // 2)
                ac.activation(w2_hi[:, part, :], w2_raw[:, part, :], ACT.Copy).then_inc(ac_w2, 1)

            for column, gate in enumerate((g_xattn, g_ffn, scale)):
                ac.dma_start(gates[:, column:column + 1], gate.partition_broadcast(P)).then_inc(ld_gates, 16)
            ac.wait_ge(pl_const, 6)
            ac.activation(warm[:, 0:1], c_eps[:, 0:1], ACT.Square).then_inc(ac_warm, 1)
            var1_step(0)
            ctx_step(0)
            ctx_step(1)
            ac.wait_ge(ld_gates, 48)
            ac.activation(tg[:, :], gates[:, 0:2], ACT.Tanh).then_inc(ac_tg, 1)
            ac.activation(warm[:, 1:2], c_eps[:, 0:1], ACT.Silu).then_inc(ac_warm, 1)
            hT_step(0)
            ctx_step(2)
            ctx_step(3)
            sq_step(0)
            sq_step(1)
            silu_step(0, 0)
            silu_step(0, 1)
            act_hi_step(0, 0)
            act_hi_step(0, 1)
            silu_step(0, 2)
            silu_step(0, 3)
            act_hi_step(0, 2)
            sq_step(2)
            act_hi_step(0, 3)
            sq_step(3)
            sq_step(4)
            sq_step(5)
            var2_step(0)
            sq_step(6)
            sq_step(7)
            mu_hi_step(0, 0)
            xT_step(0)
            mu_hi_step(0, 1)
            ssq_step(0)
            mu_hi_step(1, 0)
            mu_hi_step(1, 1)

            def iteration(b, a):
                if is_first(b):
                    w2_hi_step(0)
                    w1_hi_step(0)
                    w1_hi_step(1)
                    mu_hi_step(2, 0)
                    mu_hi_step(2, 1)
                    w2_hi_step(1)
                    ac.wait_ge(ld_b2, 48)
                    ac.activation(b2_parts[:, :], b2_raw[:, :], ACT.Copy).then_inc(ac_b2, 1)
                if a is not None:
                    var1_step(a)
                exp1(b, 0)
                exp1(b, 1)
                if is_first(b):
                    mu_hi_step(3, 0)
                    mu_hi_step(3, 1)
                exp1(b, 2)
                exp1(b, 3)
                disp_step(b, 0)
                if a is not None:
                    hT_step(a)
                exp1(b, 4)
                exp1(b, 5)
                G_step(b, 0)
                G_step(b, 1)
                disp_step(b, 1)
                exp1(b, 6)
                exp1(b, 7)
                exp2(b, 0, 0)
                exp2(b, 0, 1)
                disp_step(b, 2)
                exp2(b, 1, 0)
                exp2(b, 1, 1)
                G_step(b, 2)
                G_step(b, 3)
                exp2(b, 2, 0)
                exp2(b, 2, 1)
                disp_step(b, 3)
                exp2(b, 3, 0)
                exp2(b, 3, 1)
                if a is not None:
                    silu_step(a, 0)
                    silu_step(a, 1)
                    act_hi_step(a, 0)
                    act_hi_step(a, 1)
                    silu_step(a, 2)
                    silu_step(a, 3)
                    act_hi_step(a, 2)
                    cT_step(b, 0)
                    act_hi_step(a, 3)
                    cT_step(b, 1)
                    gelu_step(b, 0)
                    h_hi_step(b, 0)
                    cT_step(b, 2)
                    cT_step(b, 3)
                else:
                    gelu_step(b, 0)
                    h_hi_step(b, 0)
                    for g in range(4):
                        cT_step(b, g)
                gelu_step(b, 1)
                h_hi_step(b, 1)
                Q_step(b, 0)
                cT_step(b, 4)
                cT_step(b, 5)
                Q_step(b, 1)
                if a is not None:
                    var2_step(a)
                cT_step(b, 6)
                cT_step(b, 7)
                sT_step(b)
                Q_step(b, 2)
                if a is not None:
                    ssq_step(a)
                Q_step(b, 3)
                if a is not None:
                    xT_step(a)

            iteration(0, 1)
            with ac.Fori(1, B - 1) as b:
                iteration(b, b + 1)
            iteration(B - 1, None)

        @block.vector
        def _(dv):
            def split_lo(out_lo, whole, hi):
                return dv.tensor_tensor(out_lo, whole, as_f32(hi), ALU.subtract)

            def centre1(a):
                dv.wait_ge(pe_xT, nth(a, 1, -1))
                if is_first(a):
                    dv.wait_ge(ld_x0, 16)
                else:
                    dv.wait_ge(ld_x, 16 * (B - 1))
                for nt in range(NT):
                    dv.tensor_scalar(xc[:, nt, :], token_tile(a, nt), 1.0 / D, None, ALU.mult, ALU.add,
                                     accum_out=mean1[:, nt:nt + 1]).then_inc(dv_mean1, 1)
                for nt in range(NT):
                    dv.wait_ge(dv_mean1, nth(a, NT, nt))
                    dv.tensor_scalar(xc[:, nt, :], token_tile(a, nt), mean1[:, nt:nt + 1], None,
                                     ALU.subtract).then_inc(dv_xc1, 1)

            def pick_step(a):
                dv.wait_ge(dv_x1, nth(a, E * NT, -1))
                dv.wait_ge(dv_cls, E - 1)
                for e in range(E):
                    dv.tensor_scalar(pick[:, e, :], cls[:, bass.ds(a * NT, NT)], e, None,
                                     ALU.is_equal).then_inc(dv_pick, 1)
                dv.wait_ge(ac_tg, 1)
                dv.wait_ge(dv_pick, nth(a, E + 1, E - 1))
                dv.tensor_scalar(pick[:, :, :], pick[:, :, :], tg[:, 0:1], None, ALU.mult).then_inc(dv_pick, 1)

            def norm1(a):
                dv.wait_ge(ac_var1, nth(a, NT, NT - 1))
                dv.wait_ge(pl_rstd1, nth(a, 2, 1))
                for nt in range(NT):
                    dv.tensor_scalar(xc[:, nt, :], xc[:, nt, :], rstd1[:, 1, nt:nt + 1], None,
                                     ALU.mult).then_inc(dv_hn, 1)

            def hT_step(a):
                dv.wait_ge(ac_hT, a + 1)
                split_lo(hT_lo[:, :], used(HT_BANK), hT_hi[:, :]).then_inc(dv_hT, 1)

            def act_step(a, e):
                dv.wait_ge(ac_silu, nth(a, E, e))
                dv.tensor_tensor(act[:, e % 2, :], used(U_BANK[e]), act[:, e % 2, :], ALU.mult).then_inc(dv_act, 1)

            def act_lo_step(a, e):
                dv.wait_ge(ac_act, nth(a, E, e))
                split_lo(act_lo[:, e % 2, :], act[:, e % 2, :], act_hi[:, e % 2, :]).then_inc(dv_actlo, 1)

            def add_y(a, e, tiles=range(NT)):
                dv.wait_ge(dv_pick, nth(a, E + 1, E))
                dv.wait_ge(pe_y, nth(a, E, e))
                for nt in tiles:
                    if e:
                        dv.wait_ge(dv_x1, nth(a, E * NT, (e - 1) * NT + nt))
                    dv.scalar_tensor_tensor(out=token_tile(a, nt), in0=bank[Y_BANK[e]][:, nt * D:(nt + 1) * D],
                                            scalar=pick[:, e, nt:nt + 1], in1=token_tile(a, nt),
                                            op0=ALU.mult, op1=ALU.add,
                                            **(dict(accum_out=sum2[:, 0, nt:nt + 1]) if e == E - 1 else {})
                                            ).then_inc(dv_x1, 1)

            def centre2(a):
                dv.wait_ge(dv_x1, nth(a, E * NT, E * NT - 1))
                dv.tensor_scalar(sum2[:, 1, :], sum2[:, 0, :], -1.0 / D, None, ALU.mult).then_inc(dv_nm2, 1)
                dv.wait_ge(dv_nm2, a + 1)
                for nt in range(NT):
                    dv.tensor_scalar(xc[:, nt, :], token_tile(a, nt), sum2[:, 1, nt:nt + 1], None,
                                     ALU.add).then_inc(dv_xc2, 1)

            def x_ln_step(a):
                dv.wait_ge(ac_var2, nth(a, NT, NT - 1))
                dv.wait_ge(pl_rstd2, nth(a, 2, 1))
                for nt in range(NT):
                    dv.scalar_tensor_tensor(out=xc[:, nt, :], in0=xc[:, nt, :], scalar=rstd2[:, 1, nt:nt + 1],
                                            in1=gam[:, :], op0=ALU.mult, op1=ALU.mult).then_inc(dv_xg, 1)
                for nt in range(NT):
                    dv.wait_ge(dv_xg, nth(a, NT, nt))
                    dv.tensor_tensor(xc[:, nt, :], xc[:, nt, :], bet[:, :], ALU.add).then_inc(dv_xln, 1)

            def ssg_step(a):
                dv.wait_ge(ac_ssq, nth(a, NT, NT - 1))
                dv.wait_ge(pl_rn, nth(a, 2, -1))
                dv.tensor_scalar(ssg[:, :], ssq[:, :], L2_EPS * L2_EPS, None, ALU.max).then_inc(dv_ssg, 1)

            def xT_step(a):
                dv.wait_ge(ac_xT, a + 1)
                split_lo(xT_lo[:, :], used(XT_BANK), xT_hi[:, :]).then_inc(dv_xT, 1)

            def logits(b, j):
                c, nt = j // 2, j % 2
                dv.wait_ge(pl_rn, nth(b, 2, 1))
                dv.wait_ge(pe_T3, nth(b, NG, -1))
                dv.wait_ge(dv_es, nth(b, NCH, -1))
                if is_first(b):
                    dv.wait_ge(*mu_lo_done(c))
                dv.wait_ge(pe_L, nth(b, 2 * NCH, j))
                dv.tensor_scalar(lg[:, nt, c * CW:(c + 1) * CW], used(j % 2), rnorm[:, 1, nt:nt + 1], None,
                                 ALU.mult, ALU.max, accum_out=mx[:, nt, c:c + 1]).then_inc(dv_L, 1)

            def max_s(b, g):
                dv.wait_ge(ac_exp1, nth(b, NG, -1))
                dv.wait_ge(pe_T1, nth(b, NG, g))
                dv.tensor_reduce(nmax_s[:, 2 * g:2 * g + 2], used(2 + g % 2).rearrange("p (j n) -> p j n", j=2),
                                 axis=AX.X, op=ALU.max, negate=True).then_inc(dv_M1, 1)

            def max_n(b):
                dv.wait_ge(dv_L, nth(b, 2 * NCH, 2 * NCH - 1))
                dv.tensor_reduce(nmax_n[:, :], mx[:, :, :], axis=AX.X, op=ALU.max, negate=True).then_inc(dv_M2, 1)

            def disp_step(b, c):
                dv.wait_ge(pe_T2, nth(b, 2 * NCH, 2 * c + 1))
                dv.wait_ge(pe_h, nth(b, NCH, c - 2) if c >= 2 else nth(b, NCH, -1))
                if is_first(b):
                    dv.wait_ge(pl_w2, 4)
                dv.tensor_copy(disp[:, c % 2, 1, :], used(5)).then_inc(dv_disp, 1)

            def rZ_step(b, q):
                dv.wait_ge(ac_exp1, nth(b, NG, 4 * q + 3))
                dv.wait_ge(dv_hs, nth(b, 2, -1))
                half = slice(8 * q, 8 * q + 8)
                dv.reciprocal(rZ_s[:, half], Z_s[:, half]).then_inc(dv_rZ, 1)

            def hidden_scale(b, q):
                dv.wait_ge(dv_rZ, nth(b, 2, q))
                dv.wait_ge(dv_hlo, nth(b, 2, -1))
                dv.wait_ge(pe_h, nth(b, NCH, 2 * q + 1))
                dv.tensor_tensor(hid[:, q, :].rearrange("p (e h) -> p e h", h=H),
                                 used(6 + q).rearrange("p (e h) -> p e h", h=H),
                                 rZ_s[:, 8 * q:8 * q + 8].unsqueeze(2).to_broadcast([P, 8, H]),
                                 ALU.mult).then_inc(dv_hs, 1)

            def hidden_lo(b, q):
                dv.wait_ge(ac_h, nth(b, 2, q))
                split_lo(h_lo[:, 4 * q:4 * q + 4, 0:4:3, :], hid[:, q, :].rearrange("p (j t h) -> p j t h", t=2, h=H),
                         h_hi[:, 4 * q:4 * q + 4, 0:4:3, :]).then_inc(dv_hlo, 1)

            def esum_step(b, c):
                dv.wait_ge(ac_exp2, nth(b, 2 * NCH, 2 * c + 1))
                dv.wait_ge(dv_ep, nth(b, 2, -1))
                dv.wait_ge(dv_Zn, nth(b, 3, -1))
                dv.tensor_reduce(esum[:, :, c * EPC:(c + 1) * EPC],
                                 lg[:, :, c * CW:(c + 1) * CW].rearrange("p t (e s) -> p t e s", s=S),
                                 axis=AX.X, op=ALU.add).then_inc(dv_es, 1)

            def esum_split(b):
                dv.wait_ge(dv_es, nth(b, NCH, NCH - 1))
                dv.wait_ge(pe_sT, nth(b, 1, -1))
                dv.tensor_copy(esum_parts[:, :, 0:2 * GR].rearrange("p t (i e) -> p t i e", e=GR)[:, :, :, 0:E2],
                               esum[:, :, :].unsqueeze(2).to_broadcast([P, NT, 2, E2])).then_inc(dv_ep, 1)
                dv.wait_ge(dv_ep, nth(b, 2, 0))
                split_lo(esum_parts[:, :, 2 * GR:2 * GR + E2], esum[:, :, :],
                         esum_parts[:, :, 0:E2]).then_inc(dv_ep, 1)

            def b2_lo_step():
                dv.wait_ge(ac_b2, 1)
                rows = slice(GR, GR + E2)
                split_lo(b2_parts[rows, :], b2_raw[rows, :], b2_parts[rows, :]).then_inc(dv_b2, 1)

            def Zn_step(b):
                dv.wait_ge(dv_es, nth(b, NCH, NCH - 1))
                dv.wait_ge(dv_fin, nth(b, NT, -1))
                dv.tensor_reduce(Z_n[:, 0, :], esum[:, :, :], axis=AX.X, op=ALU.add).then_inc(dv_Zn, 1)
                dv.wait_ge(dv_Zn, nth(b, 3, 0))
                dv.reciprocal(Z_n[:, 1, :], Z_n[:, 0, :]).then_inc(dv_Zn, 1)
                dv.wait_ge(dv_Zn, nth(b, 3, 1))
                dv.tensor_scalar(Z_n[:, 2, :], Z_n[:, 1, :], tg[:, 1:2], None, ALU.mult).then_inc(dv_Zn, 1)

            def cT_step(b, g):
                dv.wait_ge(ac_cT, nth(b, NG, g))
                split_lo(cT_lo[:, g % 4, :, :].rearrange("p j n -> p (j n)"), used(T3_BANK[g % 4]),
                         cT_hi[:, g % 4, :, :].rearrange("p j n -> p (j n)")).then_inc(dv_cT, 1)

            def Q_step(b, c):
                dv.wait_ge(ac_Q, nth(b, NCH, c))
                split_lo(qT_lo[:, c % 2, :], used(c % 2), qT_hi[:, c % 2, :]).then_inc(dv_Q, 1)

            def final(b):
                dv.wait_ge(dv_Zn, nth(b, 3, 2))
                for nt in range(NT):
                    dv.wait_ge(pe_out, nth(b, NCH * NT, NT * (NCH - 1) + nt))
                    dv.scalar_tensor_tensor(out=token_tile(b, nt), in0=used(6 + nt, D), scalar=Z_n[:, 2, nt:nt + 1],
                                            in1=token_tile(b, nt), op0=ALU.mult, op1=ALU.add).then_inc(dv_fin, 1)

            def mu_lo_step(c, k):
                dv.wait_ge(ac_mu, DK * c + k + 1)
                part = slice(c * CW, (c + 1) * CW)
                split_lo(mu_lo[:, k, part], mu_raw[:, k, part], mu_hi[:, k, part]).then_inc(dv_mu, 1)

            def ctx_lo_step(e):
                dv.wait_ge(ac_ctx, e + 1)
                part = slice(e * F, (e + 1) * F)
                split_lo(ctxT_lo[:, :, part], used(2 + e % 2).rearrange("p (k f) -> p k f", k=DK),
                         ctxT_hi[:, :, part]).then_inc(dv_ctx, 1)

            def class_step(e):
                if e == 1:
                    dv.wait_ge(dv_ids, 1)
                    dv.tensor_scalar(cls[:, :], ids_f[:, :], PER_EXPERT, None, ALU.is_ge).then_inc(dv_cls, 1)
                else:
                    dv.wait_ge(dv_cls, e - 1)
                    dv.scalar_tensor_tensor(out=cls[:, :], in0=ids_f[:, :], scalar=e * PER_EXPERT,
                                            in1=cls[:, :], op0=ALU.is_ge, op1=ALU.add).then_inc(dv_cls, 1)

            def mun_step(c, k):
                dv.wait_ge(ac_sq, DK * c + k + 1)
                dv.wait_ge(pe_mu_bc, c + 1)
                part = mu_raw[:, k, c * CW:(c + 1) * CW]
                dv.tensor_tensor(part, used(MU_BC_BANK[c]), part, ALU.mult).then_inc(dv_mun, 1)

            def mu_ss_step(c):
                part = slice(c * EPC, (c + 1) * EPC)
                dv.wait_ge(pe_mu_ss, c + 1)
                dv.tensor_scalar(mu_ss[:, 0, part], bank[MU_SS_BANK[c]][:, part], L2_EPS * L2_EPS, None,
                                 ALU.max).then_inc(dv_mu_ss, 1)

            centre1(0)
            norm1(0)
            ctx_lo_step(0)
            ctx_lo_step(1)
            hT_step(0)
            ctx_lo_step(2)
            ctx_lo_step(3)
            dv.wait_ge(ld_ids, 16)
            dv.tensor_copy(ids_f, ids_raw.bitcast(I32)).then_inc(dv_ids, 1)
            for e in range(1, E):
                class_step(e)
            pick_step(0)
            act_step(0, 0)
            act_step(0, 1)
            act_lo_step(0, 0)
            act_lo_step(0, 1)
            act_step(0, 2)
            act_step(0, 3)
            act_lo_step(0, 2)
            add_y(0, 0)
            act_lo_step(0, 3)
            add_y(0, 1)
            mu_ss_step(0)
            add_y(0, 2)
            add_y(0, 3)
            centre2(0)
            mu_ss_step(1)
            mun_step(0, 0)
            dv.wait_ge(ld_rows, 32)
            x_ln_step(0)
            mun_step(0, 1)
            mu_ss_step(2)
            mu_lo_step(0, 0)
            xT_step(0)
            mu_lo_step(0, 1)
            ssg_step(0)
            mun_step(1, 0)
            mun_step(1, 1)

            def iteration(b, a):
                logits(b, 0)
                logits(b, 1)
                if is_first(b):
                    for k in range(DK):
                        mun_step(2, k)
                    mu_ss_step(3)
                if a is not None:
                    centre1(a)
                logits(b, 2)
                logits(b, 3)
                max_s(b, 0)
                max_s(b, 1)
                if a is not None and not is_first(b):
                    norm1(a)
                logits(b, 4)
                if is_first(b):
                    for k in range(DK):
                        mun_step(3, k)
                logits(b, 5)
                if is_first(b):
                    for k in range(DK):
                        mu_lo_step(3, k)
                    norm1(a)
                max_s(b, 2)
                max_s(b, 3)
                disp_step(b, 0)
                logits(b, 6)
                logits(b, 7)
                if a is not None:
                    hT_step(a)
                max_s(b, 4)
                max_s(b, 5)
                max_n(b)
                if is_first(b):
                    b2_lo_step()
                disp_step(b, 1)
                rZ_step(b, 0)
                max_s(b, 6)
                max_s(b, 7)
                disp_step(b, 2)
                esum_step(b, 0)
                hidden_scale(b, 0)
                rZ_step(b, 1)
                esum_step(b, 1)
                if a is not None:
                    pick_step(a)
                disp_step(b, 3)
                esum_step(b, 2)
                if a is None:
                    esum_step(b, 3)
                if a is not None:
                    act_step(a, 0)
                    act_step(a, 1)
                    act_lo_step(a, 0)
                    act_lo_step(a, 1)
                hidden_scale(b, 1)
                if a is not None:
                    esum_step(b, 3)
                    act_step(a, 2)
                    act_step(a, 3)
                    add_y(a, 0)
                    act_lo_step(a, 2)
                    add_y(a, 1)
                    act_lo_step(a, 3)
                else:
                    hidden_lo(b, 0)
                cT_step(b, 0)
                cT_step(b, 1)
                if a is not None:
                    add_y(a, 2)
                    hidden_lo(b, 0)
                cT_step(b, 2)
                cT_step(b, 3)
                if a is not None:
                    add_y(a, 3)
                hidden_lo(b, 1)
                Q_step(b, 0)
                if a is not None:
                    centre2(a)
                cT_step(b, 4)
                cT_step(b, 5)
                Q_step(b, 1)
                esum_split(b)
                cT_step(b, 6)
                cT_step(b, 7)
                if a is not None:
                    x_ln_step(a)
                Q_step(b, 2)
                if a is not None:
                    ssg_step(a)
                Zn_step(b)
                Q_step(b, 3)
                if a is not None:
                    xT_step(a)
                final(b)

            iteration(0, 1)
            with dv.Fori(1, B - 1) as b:
                iteration(b, b + 1)
            iteration(B - 1, None)

        @block.tensor
        def _(pe):
            def mm(out_ap, lhsT, rhs, start, stop):
                return pe.matmul(out_ap, lhsT, rhs, start=start, stop=stop, skip_group_check=True)

            def mm_split(out_ap, lhs, rhs, start, stop):
                mm(out_ap, lhs[0], rhs[0], start, False)
                mm(out_ap, lhs[0], rhs[1], False, False)
                return mm(out_ap, lhs[1], rhs[0], False, stop)

            def hT_transposes(a):
                pe.wait_ge(pl_ident, 1)
                for nt in range(NT):
                    pe.wait_ge(dv_hn, nth(a, NT, nt))
                    for k in range(DK):
                        last = pe.transpose(bank[HT_BANK][:, k * N + nt * P:k * N + (nt + 1) * P],
                                            xc[:, nt, k * P:(k + 1) * P], ident[:, :])
                last.then_inc(pe_hT, 1)

            def u_step(a, e):
                if e == 0:
                    pe.wait_ge(ac_hT, a + 1)
                    pe.wait_ge(dv_hT, a + 1)
                for f in range(2):
                    for k in range(DK):
                        cols = slice(e * F + f * P, e * F + (f + 1) * P)
                        rows = slice(k * N, (k + 1) * N)
                        last = mm_split(bank[U_BANK[e]][:, f * N:(f + 1) * N],
                                        (ctxT_hi[:, k, cols], ctxT_lo[:, k, cols]),
                                        (hT_hi[:, rows], hT_lo[:, rows]), k == 0, k == DK - 1)
                last.then_inc(pe_u, 1)

            def y_step(a, e):
                pe.wait_ge(ac_act, nth(a, E, e))
                pe.wait_ge(dv_actlo, nth(a, E, e))
                if e >= 2:
                    pe.wait_ge(dv_x1, nth(a, E * NT, (e - 2) * NT + NT - 1))
                for nt in range(NT):
                    for f in range(2):
                        tok = slice(f * N + nt * P, f * N + (nt + 1) * P)
                        cols = slice(e * F, (e + 1) * F)
                        last = mm_split(bank[Y_BANK[e]][:, nt * D:(nt + 1) * D],
                                        (act_hi[:, e % 2, tok], act_lo[:, e % 2, tok]),
                                        (ctxT_hi[:, f, cols], ctxT_lo[:, f, cols]), f == 0, f == 1)
                last.then_inc(pe_y, 1)

            def xT_transposes(a):
                for nt in range(NT):
                    pe.wait_ge(dv_xln, nth(a, NT, nt))
                    for k in range(DK):
                        last = pe.transpose(bank[XT_BANK][:, k * N + nt * P:k * N + (nt + 1) * P],
                                            xc[:, nt, k * P:(k + 1) * P], ident[:, :])
                last.then_inc(pe_xT, 1)

            def x_rows(k, nt):
                rows = slice(k * N + nt * P, k * N + (nt + 1) * P)
                return xT_hi[:, rows], xT_lo[:, rows]

            def L_step(b, j):
                c, nt = j // 2, j % 2
                cols = slice(c * CW, (c + 1) * CW)
                if is_first(b):
                    pe.wait_ge(ac_mu, DK * (c + 1))
                    pe.wait_ge(*mu_lo_done(c))
                if j < 2:
                    pe.wait_ge(ac_xT, b + 1)
                    pe.wait_ge(dv_xT, b + 1)
                    pe.wait_ge(dv_Q, nth(b, NCH, -1))
                else:
                    pe.wait_ge(dv_L, nth(b, 2 * NCH, j - 2))
                for k in range(DK):
                    last = mm_split(used(j % 2), x_rows(k, nt), (mu_hi[:, k, cols], mu_lo[:, k, cols]),
                                    k == 0, k == DK - 1)
                last.then_inc(pe_L, 1)

            def G_step(b, i):
                ch, nt = i // 2, i % 2
                cols = slice(ch * CW, (ch + 1) * CW)
                if i < 2:
                    pe.wait_ge(dv_L, nth(b, 2 * NCH, 6 + i))
                else:
                    pe.wait_ge(ac_G, nth(b, 4, i - 2))
                for k in range(DK):
                    last = mm_split(used(i % 2), x_rows(k, nt), (w1_hi[:, k, cols], w1_lo[:, k, cols]),
                                    k == 0, k == DK - 1)
                last.then_inc(pe_G, 1)

            def T1_step(b, g):
                c = g // 2
                pe.wait_ge(dv_L, nth(b, 2 * NCH, 2 * c + 1))
                if g >= 2:
                    pe.wait_ge(ac_exp1, nth(b, NG, g - 2))
                else:
                    pe.wait_ge(ac_sT, nth(b, 1, -1))
                    pe.wait_ge(dv_xT, b + 1)
                for j in range(2):
                    for nt in range(NT):
                        s = (2 * g + j) * S
                        last = pe.transpose(bank[2 + g % 2][:, j * N + nt * P:j * N + (nt + 1) * P],
                                            lg[:, nt, s:s + S], ident[:, :])
                last.then_inc(pe_T1, 1)

            def T2_step(b, c):
                pe.wait_ge(ac_exp1, nth(b, NG, 2 * c + 1))
                for nt in range(NT):
                    if c == 0:
                        pe.wait_ge(dv_cT, nth(b, NG, -1))
                    else:
                        pe.wait_ge((ac_disp, dv_disp)[nt], nth(b, NCH, c - 1))
                    for j in range(EPC):
                        last = pe.transpose(bank[4 + nt][:, j * S:(j + 1) * S],
                                            dT[:, c % 2, j, nt * P:(nt + 1) * P], ident[:, :])
                    last.then_inc(pe_T2, 1)

            def h_step(b, c):
                pe.wait_ge(ac_disp, nth(b, NCH, c))
                pe.wait_ge(dv_disp, nth(b, NCH, c))
                pe.wait_ge(ac_G, nth(b, 4, 2 * (c // 2) + 1))
                pe.wait_ge(dv_fin, nth(b, NT, -1))
                for j in range(EPC):
                    e = c * EPC + j
                    for nt in range(NT):
                        last = mm(bank[6 + c // 2][:, (e % 8) * H:(e % 8 + 1) * H],
                                  disp[:, c % 2, nt, j * S:(j + 1) * S], G[:, nt, e * H:(e + 1) * H],
                                  nt == 0, nt == NT - 1)
                last.then_inc(pe_h, 1)

            def T3_step(b, a, g):
                pe.wait_ge(ac_exp2, nth(b, 2 * NCH, 2 * (g // 2) + 1))
                if g >= 4:
                    pe.wait_ge(dv_cT, nth(b, NG, g - 4))
                elif g < 2:
                    pe.wait_ge(ac_exp1, nth(b, NG, 6 + g))
                elif a is not None:
                    pe.wait_ge(dv_act, nth(a, E, g))
                else:
                    pe.wait_ge((ac_disp, dv_disp)[g % 2], nth(b, NCH, NCH - 1))
                for j in range(2):
                    for nt in range(NT):
                        s = (2 * g + j) * S
                        last = pe.transpose(bank[T3_BANK[g % 4]][:, j * N + nt * P:j * N + (nt + 1) * P],
                                            lg[:, nt, s:s + S], ident[:, :])
                last.then_inc(pe_T3, 1)

            def Q_step(b, c):
                pe.wait_ge(ac_h, nth(b, 2, c // 2))
                pe.wait_ge(dv_hlo, nth(b, 2, c // 2))
                pe.wait_ge(dv_cT, nth(b, NG, 2 * c + 1))
                if c >= 2:
                    pe.wait_ge(dv_Q, nth(b, NCH, c - 2))
                for i in range(2):
                    p = 2 * c + i
                    for t in range(2):
                        lhs = [w[:, p, 2 * t:2 * t + 2, :].rearrange("p a h -> p (a h)") for w in (h_hi, h_lo)]
                        last = mm_split(bank[c % 2][:, i * N:(i + 1) * N], lhs,
                                        (cT_hi[:, p % 4, t, :], cT_lo[:, p % 4, t, :]), t == 0, t == 1)
                last.then_inc(pe_Q, 1)

            def sT_transposes(b):
                pe.wait_ge(dv_ep, nth(b, 2, 1))
                pe.wait_ge(dv_cT, nth(b, NG, 4))
                for nt in range(NT):
                    last = pe.transpose(bank[ST_BANK][:, nt * P:(nt + 1) * P],
                                        as_f32(esum_parts[:, nt, :]), ident[:, :])
                last.then_inc(pe_sT, 1)

            def out_step(b, c):
                pe.wait_ge(ac_Q, nth(b, NCH, c))
                pe.wait_ge(dv_Q, nth(b, NCH, c))
                if c == NCH - 1:
                    pe.wait_ge(ac_sT, b + 1)
                for nt in range(NT):
                    if c == NCH - 1:
                        mm(used(6 + nt, D), esumT[:, nt * P:(nt + 1) * P], b2_parts[:, :], False, False)
                    for i in range(2):
                        p = 2 * c + i
                        rows = slice(i * N + nt * P, i * N + (nt + 1) * P)
                        last = mm_split(used(6 + nt, D), (qT_hi[:, c % 2, rows], qT_lo[:, c % 2, rows]),
                                        (w2_hi[:, p, :], w2_lo[:, p, :]), p == 0, p == NG - 1)
                    last.then_inc(pe_out, 1)

            def ctx_transposes(e):
                pe.wait_ge(pl_ident, 1)
                pe.wait_ge(ld_ctx[e], 16)
                if e >= 2:
                    pe.wait_ge(dv_ctx, e - 1)
                for f in range(2):
                    for k in range(DK):
                        last = pe.transpose(bank[2 + e % 2][:, k * F + f * P:k * F + (f + 1) * P],
                                            ctx_raw[:, e * 2 + f, k * P:(k + 1) * P], ident[:, :])
                last.then_inc(pe_ctxT, 1)

            def mu_squares(c):
                pe.wait_ge(pl_const, 6)
                pe.wait_ge(ac_sq, DK * (c + 1))
                if c == 0:
                    pe.wait_ge(dv_ctx, E)
                elif c < 3:
                    pe.wait_ge(dv_act, c)
                else:
                    pe.wait_ge(dv_x1, 3 * NT)
                for j in range(EPC):
                    s = c * EPC + j
                    for k in range(DK):
                        last = mm(bank[MU_SS_BANK[c]][:, s:s + 1],
                                  mu_sq[:, k, (c % 2) * CW + j * P:(c % 2) * CW + (j + 1) * P], ones[:, 0:1],
                                  k == 0, k == DK - 1)
                last.then_inc(pe_mu_ss, 1)

            def mu_spread(c):
                pe.wait_ge(pl_diag, c + 1)
                if c in (1, 2):
                    pe.wait_ge(dv_act, c + 2)
                if c == 3:
                    pe.wait_ge(dv_x1, E * NT)
                mm(used(MU_BC_BANK[c]), ones[:, :], hid[:, c % 2, :], True, True).then_inc(pe_mu_bc, 1)

            def ctx_ready(e):
                pe.wait_ge(ac_ctx, e + 1)
                pe.wait_ge(dv_ctx, e + 1)

            ctx_transposes(0)
            ctx_transposes(1)
            hT_transposes(0)
            ctx_transposes(2)
            ctx_transposes(3)
            ctx_ready(0)
            u_step(0, 0)
            ctx_ready(1)
            u_step(0, 1)
            ctx_ready(2)
            u_step(0, 2)
            ctx_ready(3)
            u_step(0, 3)
            y_step(0, 0)
            y_step(0, 1)
            mu_squares(0)
            y_step(0, 2)
            y_step(0, 3)
            mu_spread(0)
            mu_squares(1)
            mu_squares(2)
            xT_transposes(0)
            mu_spread(1)
            pe.wait_ge(dv_mu_ss, 3)

            def iteration(b, a):
                L_step(b, 0)
                L_step(b, 1)
                if is_first(b):
                    mu_spread(2)
                    mu_squares(3)
                L_step(b, 2)
                L_step(b, 3)
                T1_step(b, 0)
                T1_step(b, 1)
                L_step(b, 4)
                if is_first(b):
                    mu_spread(3)
                L_step(b, 5)
                T1_step(b, 2)
                T1_step(b, 3)
                T2_step(b, 0)
                L_step(b, 6)
                L_step(b, 7)
                if a is not None:
                    hT_transposes(a)
                T1_step(b, 4)
                T1_step(b, 5)
                T2_step(b, 1)
                if is_first(b):
                    pe.wait_ge(ac_w1, DK)
                    pe.wait_ge(pl_w1, DK)
                G_step(b, 0)
                G_step(b, 1)
                T1_step(b, 6)
                T1_step(b, 7)
                if a is not None:
                    pe.wait_ge(dv_hT, a + 1)
                h_step(b, 0)
                T2_step(b, 2)
                G_step(b, 2)
                G_step(b, 3)
                h_step(b, 1)
                T2_step(b, 3)
                pe.wait_ge(ac_G, nth(b, 4, 3))
                if a is not None:
                    u_step(a, 0)
                    u_step(a, 1)
                h_step(b, 2)
                h_step(b, 3)
                pe.wait_ge(dv_disp, nth(b, NCH, NCH - 1))
                if a is not None:
                    u_step(a, 2)
                    u_step(a, 3)
                T3_step(b, a, 0)
                T3_step(b, a, 1)
                pe.wait_ge(dv_hs, nth(b, 2, 1))
                if a is not None:
                    y_step(a, 0)
                    y_step(a, 1)
                T3_step(b, a, 2)
                T3_step(b, a, 3)
                if a is not None:
                    y_step(a, 2)
                    y_step(a, 3)
                T3_step(b, a, 4)
                T3_step(b, a, 5)
                Q_step(b, 0)
                Q_step(b, 1)
                T3_step(b, a, 6)
                T3_step(b, a, 7)
                if a is not None:
                    pe.wait_ge(dv_x1, nth(a, E * NT, E * NT - 1))
                if is_first(b):
                    pe.wait_ge(ac_w2, 2)
                    pe.wait_ge(pl_w2, 4)
                    pe.wait_ge(dv_b2, 1)
                out_step(b, 0)
                Q_step(b, 2)
                sT_transposes(b)
                out_step(b, 1)
                Q_step(b, 3)
                if a is not None:
                    pe.wait_ge(dv_cT, nth(b, NG, 5))
                    xT_transposes(a)
                out_step(b, 2)
                out_step(b, 3)

            iteration(0, 1)
            with pe.Fori(1, B - 1) as b:
                iteration(b, b + 1)
            iteration(B - 1, None)


_INS = ["x", "itok_BxS_13_99985", "ctx_2048", "g_xattn", "g_ffn", "L0_ffn_gamma", "L0_ffn_beta", "L0_ffn_mu",
        "L0_ffn_scale", "L0_ffn_W1", "L0_ffn_b1", "L0_ffn_W2", "L0_ffn_b2"]


def kernel(**inputs):
    import numpy as np
    import concourse.bacc as bacc
    from concourse.bass_utils import run_bass_kernel_spmd

    nc = bacc.Bacc("TRN2", target_bir_lowering=False, num_devices=1)
    arrays, args = {}, []
    for name in _INS:
        a = np.ascontiguousarray(inputs[name])
        if name.startswith("itok"):
            a = np.ascontiguousarray(a.reshape(-1, P).T)
        arrays[f"in_{name}"] = a
        args.append(nc.dram_tensor(f"in_{name}", a.shape, mybir.dt.from_np(a.dtype), kind="ExternalInput").ap())
    out = nc.dram_tensor("out_x", inputs["x"].shape, F32, kind="ExternalOutput").ap()
    flamingo_kernel(nc, *args, out)
    r = run_bass_kernel_spmd(nc, [arrays], core_ids=[0])
    return r.results[0]["out_x"]
```
